# Optimizing a Trainium2 kernel written in Bass

```python
import numpy as np
import jax
import jax.numpy as jnp

def _softmax(x, axis=-1):
    return jax.nn.softmax(x, axis=axis)

def _gelu(x):
    return jax.nn.gelu(x, approximate=True)

def _silu(x):
    return jax.nn.silu(x)

def _sigmoid(x):
    return jax.nn.sigmoid(x)

def _layernorm(x, axis=-1, eps=1e-05):
    m = jnp.mean(x, axis=axis, keepdims=True)
    v = jnp.var(x, axis=axis, keepdims=True)
    return (x - m) / jnp.sqrt(v + eps)

def _scatter_add(tgt, idx, src, axis=0):
    return tgt.at[idx].add(src)

def _segment_sum(src, seg, n):
    return jax.ops.segment_sum(src, seg, n)
kernel_name = 'mk_early_fusion_d1_tok_img512_r4_da41ed'

def setup_inputs(seed: int=0):
    np.random.seed(seed)
    _w = jnp.asarray

    def _rec_inputs():
        import jax
        import jax.numpy as jnp
        _rk = jax.random.key(seed)
        x = -0.000178447 + 0.99995 * jax.random.normal(jax.random.fold_in(_rk, 1), (128, 3, 176, 208), jnp.float32)
        txt = -0.051393 + 1.14128 * jax.random.normal(jax.random.fold_in(_rk, 2), (128, 32, 128), jnp.float32)
        return (x, txt)
    x, txt = _rec_inputs()

    def _L0_tok_setup():
        import jax, jax.numpy as jnp
        import numpy as np
        P1, P2, C = (16, 16, 3)
        PW, PH = (176 // P1, 208 // P2)
        key = jax.random.key(seed)
        k1, k2, k3, k4, k5 = jax.random.split(key, 5)
        B, D = (64, 128)
        patch_dim = P1 * P2 * C
        return {'x': jax.random.normal(k1, (B, C, PW * P1, PH * P2), dtype=jnp.float32), 'W': jax.random.normal(k2, (D, patch_dim), dtype=jnp.float32) * 0.02, 'b': jax.random.normal(k3, (D,), dtype=jnp.float32) * 0.02, 'cls_token': jax.random.uniform(k4, (1, 1, D), dtype=jnp.float32), 'pos_emb': jax.random.normal(k5, (1, PW * PH + 1, 1), dtype=jnp.float32)}
    _L0_tok_all = _L0_tok_setup()
    _L0_tok_in = {k: v for k, v in _L0_tok_all.items() if k in ('W', 'b', 'cls_token', 'pos_emb')}
    del _L0_tok_all

    def _L0_attn_setup():
        import jax, jax.numpy as jnp
        import numpy as np
        B, N, D_IN = (8, 512, 128)
        H = 256
        D_EMB = 128
        D_ATTN = 64
        key = jax.random.key(seed)
        ks = jax.random.split(key, 9)
        s = lambda fi, fo: (2.0 / (fi + fo)) ** 0.5
        return {'x': jax.random.normal(ks[0], (B, N, D_IN), dtype=jnp.float32), 'We1': jax.random.normal(ks[1], (D_IN, H), dtype=jnp.float32) * s(D_IN, H), 'be1': jnp.zeros((H,), dtype=jnp.float32), 'We2': jax.random.normal(ks[2], (H, D_EMB), dtype=jnp.float32) * s(H, D_EMB), 'be2': jnp.zeros((D_EMB,), dtype=jnp.float32), 'Wk1': jax.random.normal(ks[3], (D_IN, H), dtype=jnp.float32) * s(D_IN, H), 'bk1': jnp.zeros((H,), dtype=jnp.float32), 'Wk2': jax.random.normal(ks[4], (H, 2 * D_ATTN), dtype=jnp.float32) * s(H, 2 * D_ATTN), 'bk2': jnp.zeros((2 * D_ATTN,), dtype=jnp.float32)}
    _L0_attn_all = _L0_attn_setup()
    _L0_attn_in = {k: v for k, v in _L0_attn_all.items() if k in ('We1', 'be1', 'We2', 'be2', 'Wk1', 'bk1', 'Wk2', 'bk2')}
    del _L0_attn_all

    def _L0_ffn_setup():
        import jax, jax.numpy as jnp
        import numpy as np
        B, T, D = (4, 2048, 128)
        E, F, CAP = (8, 512, 1024)
        key = jax.random.key(seed)
        ks = jax.random.split(key, 6)
        s = 0.02
        return {'x': jax.random.normal(ks[0], (B, T, D), dtype=jnp.float32), 'Wr': jax.random.normal(ks[1], (D, E), dtype=jnp.float32) * s, 'W1': jax.random.normal(ks[2], (E, D, F), dtype=jnp.float32) * s, 'b1': jax.random.normal(ks[3], (E, F), dtype=jnp.float32) * s, 'W2': jax.random.normal(ks[4], (E, F, D), dtype=jnp.float32) * s, 'b2': jax.random.normal(ks[5], (E, D), dtype=jnp.float32) * s}
    _L0_ffn_all = _L0_ffn_setup()
    _L0_ffn_in = {k: v for k, v in _L0_ffn_all.items() if k in ('Wr', 'W1', 'b1', 'W2', 'b2')}
    del _L0_ffn_all
    return {'x': x, 'txt': txt, 'L0_tok_W': _L0_tok_in['W'], 'L0_tok_b': _L0_tok_in['b'], 'L0_tok_cls_token': _L0_tok_in['cls_token'], 'L0_tok_pos_emb': _L0_tok_in['pos_emb'], 'L0_attn_We1': _L0_attn_in['We1'], 'L0_attn_be1': _L0_attn_in['be1'], 'L0_attn_We2': _L0_attn_in['We2'], 'L0_attn_be2': _L0_attn_in['be2'], 'L0_attn_Wk1': _L0_attn_in['Wk1'], 'L0_attn_bk1': _L0_attn_in['bk1'], 'L0_attn_Wk2': _L0_attn_in['Wk2'], 'L0_attn_bk2': _L0_attn_in['bk2'], 'L0_ffn_Wr': _L0_ffn_in['Wr'], 'L0_ffn_W1': _L0_ffn_in['W1'], 'L0_ffn_b1': _L0_ffn_in['b1'], 'L0_ffn_W2': _L0_ffn_in['W2'], 'L0_ffn_b2': _L0_ffn_in['b2']}

def reference(x, txt, L0_tok_W, L0_tok_b, L0_tok_cls_token, L0_tok_pos_emb, L0_attn_We1, L0_attn_be1, L0_attn_We2, L0_attn_be2, L0_attn_Wk1, L0_attn_bk1, L0_attn_Wk2, L0_attn_bk2, L0_ffn_Wr, L0_ffn_W1, L0_ffn_b1, L0_ffn_W2, L0_ffn_b2):
    import jax
    import jax.numpy as jnp

    def _L0_tok_ref(x, W, b, cls_token, pos_emb):
        import jax, jax.numpy as jnp
        import numpy as np
        P1, P2, C = (16, 16, 3)
        PW, PH = (176 // P1, 208 // P2)
        B = x.shape[0]
        patches = x.reshape(B, C, PW, P1, PH, P2)
        patches = patches.transpose(0, 2, 4, 3, 5, 1).reshape(B, PW * PH, P1 * P2 * C)
        proj = jnp.einsum('bnp,dp->bnd', patches, W) + b
        cls = jnp.broadcast_to(cls_token, (B, 1, cls_token.shape[-1]))
        out = jnp.concatenate([cls, proj], axis=1) + pos_emb
        return out

    def _L0_attn_ref(x, We1, be1, We2, be2, Wk1, bk1, Wk2, bk2):
        import jax, jax.numpy as jnp
        import numpy as np
        B, N, D_IN = (8, 512, 128)
        H = 256
        D_EMB = 128
        D_ATTN = 64
        embs = jax.nn.relu(x @ We1 + be1) @ We2 + be2
        kq = jax.nn.relu(x @ Wk1 + bk1) @ Wk2 + bk2
        K, Q = (kq[..., :D_ATTN], kq[..., D_ATTN:])
        scores = jnp.einsum('bqd,bkd->bqk', Q, K)
        A = jax.nn.softmax(scores, axis=-1)
        return jnp.einsum('bqk,bkd->bqd', A, embs)

    def _L0_ffn_ref(x, Wr, W1, b1, W2, b2):
        import jax, jax.numpy as jnp
        import numpy as np
        B, T, D = (4, 2048, 128)
        E, F, CAP = (8, 512, 1024)
        Bb, Tt, Dd = x.shape
        N = Bb * Tt
        C = min(CAP, N)
        x_flat = x.reshape(N, Dd)
        logits = x_flat @ Wr
        probs = jax.nn.softmax(logits, axis=0)
        vals, idx = jax.lax.top_k(probs.T, C)
        selected = x_flat[idx]
        h = jax.nn.gelu(jnp.einsum('ecd,edf->ecf', selected, W1) + b1[:, None, :], approximate=False)
        out_e = jnp.einsum('ecf,efd->ecd', h, W2) + b2[:, None, :]
        weighted = vals[..., None] * out_e
        output = jnp.zeros_like(x_flat).at[idx.reshape(-1)].add(weighted.reshape(-1, Dd))
        return output.reshape(Bb, Tt, Dd)
    h = _L0_tok_ref(x, L0_tok_W, L0_tok_b, L0_tok_cls_token, L0_tok_pos_emb)
    h = jnp.concatenate([h, txt], axis=1)
    h = h + _L0_attn_ref(_layernorm(h, axis=-1), L0_attn_We1, L0_attn_be1, L0_attn_We2, L0_attn_be2, L0_attn_Wk1, L0_attn_bk1, L0_attn_Wk2, L0_attn_bk2)
    h = h + _L0_ffn_ref(_layernorm(h, axis=-1), L0_ffn_Wr, L0_ffn_W1, L0_ffn_b1, L0_ffn_W2, L0_ffn_b2)
    return h

_drawn_inputs = setup_inputs


def setup_inputs(seed=0):
    import zlib

    import numpy as np

    out = dict(_drawn_inputs(seed))
    spreads = {'L0_attn_be1': (0.0, 0.1),
     'L0_attn_be2': (0.0, 0.1),
     'L0_attn_bk1': (0.0, 0.1),
     'L0_attn_bk2': (0.0, 0.1)}
    factors = {'L0_ffn_Wr': 64.0,
     'L0_ffn_W1': 64.0,
     'L0_ffn_b1': 64.0,
     'L0_ffn_W2': 64.0,
     'L0_ffn_b2': 200.0,
     'L0_tok_cls_token': 8.0}
    for name, (base, spread) in spreads.items():
        noise = np.random.default_rng([zlib.crc32(name.encode()), seed]).standard_normal(out[name].shape)
        drawn = base * np.exp(spread * noise) if base else spread * noise
        out[name] = jnp.asarray(drawn.astype(out[name].dtype))
    for name, factor in factors.items():
        out[name] = (out[name] * factor).astype(out[name].dtype)
    return out
```

```python
import concourse.bass as bass
from concourse import mybir
from contextlib import ExitStack

IMGS = 128
PATCHES = 143
TXT = 32
TOK = 1 + PATCHES + TXT
HALF = TOK // 2
D = 128
PK = 6
PAIRS = IMGS // 2
IMG_ROWS1 = 1 + PATCHES - HALF
HID = 256
DA = 64
E = 8
F = 512
FT = F // 128
CAP = 1024
CH = CAP // 128
COLS = 2 * IMGS
BLK = COLS // 128
EPS = 1e-5
TOP_BIT = 1 << 29
BITS = 30
TW = HALF + 2


def fusion_program(nc, x, txt, tok_w, tok_b, cls, pos, w_up, b_up, w_e2, b_e2, w_kq, b_kq,
                   wr, w1, b1, w2, b2, ident, upto, after, before, rank, number, out):
    f32, bf16, i32 = mybir.dt.float32, mybir.dt.bfloat16, mybir.dt.int32
    ALU = mybir.AluOpType
    ACT = mybir.ActivationFunctionType
    AX = mybir.AxisListType

    pair_rows = out.rearrange("(t m) (c p) d -> t p (m c) d", m=2, c=2)
    rows_dram = out.rearrange("i n d -> (i n) d")

    ctx = ExitStack()
    with ctx:
        def sb(name, shape, dt=f32):
            return ctx.enter_context(nc.sbuf_tensor(name, shape, dt))

        def sem(name):
            return ctx.enter_context(nc.semaphore(name))

        ident_s = sb("ident_s", [128, 128])
        upto_s = sb("upto_s", [HALF, HALF])
        after_s = sb("after_s", [HALF, HALF])
        before_s = sb("before_s", [128, 128])
        rank_s = sb("rank_s", [128, CAP])
        number_s = sb("number_s", [128, CH + BLK])
        upto_b = sb("upto_b", [HALF, HALF], bf16)
        after_b = sb("after_b", [HALF, HALF], bf16)
        ones_b = sb("ones_b", [HALF, HALF], bf16)
        ones_s = sb("ones_s", [128, 128])
        eps_s = sb("eps_s", [128, 8])
        half_s = sb("half_s", [128, 8])
        tokw_s = sb("tokw_s", [128, PK, D])
        tokb_s = sb("tokb_s", [D, 1])
        cls_s = sb("cls_s", [D, 1])
        pos_s = sb("pos_s", [HALF, 2])
        wup_s = sb("wup_s", [D, 4, 128])
        bup_s = sb("bup_s", [128, 4])
        we2_s = sb("we2_s", [128, 2, D])
        be2_s = sb("be2_s", [128, D])
        wkq_s = sb("wkq_s", [128, 2, 128])
        bkq_s = sb("bkq_s", [128, 1])
        wr_s = sb("wr_s", [D, E])
        w1_s = sb("w1_s", [D, E, F])
        b1_s = sb("b1_s", [128, E, FT])
        w2_s = sb("w2_s", [128, E, FT, D])
        b2_s = sb("b2_s", [128, E, D])

        arena = sb("arena", [128, E * CH * 128])
        taken = [0]

        def part(shape, names):
            n = 1
            for v in shape.values():
                n *= v
            taken[0] += n
            assert taken[0] <= E * CH * 128
            return arena[:, taken[0] - n:taken[0]].rearrange(f"p ({' '.join(shape)}) -> p {names}", **shape)

        xs = part(dict(a=2, k=PK, n=2 * PATCHES), "a k n")
        hT = part(dict(a=2, m=2, n=TOK), "a m n")
        h0 = sb("h0", [HALF, 2, 2, 2, D])
        st1 = sb("st1", [HALF, 4, 6])
        mv1 = sb("mv1", [HALF, 4, 2])
        rs1 = sb("rs1", [HALF, 2, 4])
        xn = sb("xn", [HALF, 4, D])
        xnT = sb("xnT", [D, 2 * TOK])
        hid = part(dict(m=4, n=2 * TOK), "m n")
        kT = sb("kT", [DA, 2 * TOK])
        qT = sb("qT", [DA, 2 * TOK])
        emb = sb("emb", [HALF, 4, D])
        nmax = sb("nmax", [HALF, 4])
        rsum = sb("rsum", [HALF, 4])
        rinv = sb("rinv", [HALF, 4])
        prob = part(dict(c=4, n=TOK), "c n")[0:HALF]
        probT = part(dict(m=2, k=2, q=TOK), "m k q")[0:HALF]
        h1 = sb("h1", [HALF, 2, 4, D])
        st2 = sb("st2", [HALF, 4, 6])
        mv2 = sb("mv2", [HALF, 4, 2])
        rs2 = sb("rs2", [HALF, 2, 4])
        xm = sb("xm", [HALF, 4, D])
        xmT = sb("xmT", [D, 2 * TOK])
        lg = sb("lg", [HALF, E, COLS])

        pe_ = sb("pe_", [HALF, E, COLS])
        lmax = sb("lmax", [HALF, E])
        gmax = sb("gmax", [E, 1])
        gdiag = sb("gdiag", [E, E])
        ngmax = sb("ngmax", [128, E])
        psum_p = sb("psum_p", [HALF, E])
        pinv = sb("pinv", [128, E])
        thr = sb("thr", [HALF, E], i32)
        cand = sb("cand", [HALF, E], i32)
        bit = sb("bit", [HALF, 1], i32)
        cnt = sb("cnt", [HALF, E])
        keep = sb("keep", [HALF, E], i32)
        passed = sb("passed", [128, CH, HALF], bf16)
        gt = sb("gt", [HALF, E, COLS], bf16)
        eq = sb("eq", [HALF, E, COLS], bf16)
        sel = sb("sel", [HALF, E, COLS], bf16)
        need = sb("need", [HALF, E])
        zero_s = sb("zero_s", [HALF, COLS])
        scan = sb("scan", [HALF, 2, COLS])
        rk = sb("rk", [HALF, 2, COLS])
        tie = sb("tie", [HALF, 2, COLS])
        table = sb("table", [128, E, BLK, TW])
        incl = sb("incl", [128, E, BLK])
        past = sb("past", [128, BLK, CAP], bf16)
        hot = sb("hot", [128, 2, BLK, CAP])
        slot = sb("slot", [128, 2, CH])
        place = sb("place", [128, 2, CH])
        row = sb("row", [128, E, CH], i32)

        g = sb("g", [128, E * CH, D])
        st3 = sb("st3", [128, 2, CH, 6])
        mv3 = sb("mv3", [128, 2, CH, 2])
        rs3 = sb("rs3", [128, 2, 2, CH])
        gT = arena[:, :].rearrange("p (c n) -> p c n", n=128)
        val = sb("val", [128, E, CH])
        act1 = hot[:, :, :, :].rearrange("p k b (f n) -> p k (b f) n", n=512)
        y = sb("y", [128, 4, 4, D])

        B = [ctx.enter_context(nc.psum_tensor(f"bank{n}", [128, 512], f32)) for n in range(8)]

        s_w = sem("weights_loaded")
        s_w2 = sem("late_weights_loaded")
        s_const = sem("constants_made")
        s_ht0 = sem("class_column_set")
        s_x = [sem("x_loaded_0"), sem("x_loaded_1")]
        s_txt = [sem("txt_loaded_0"), sem("txt_loaded_1")]
        s_proj = sem("proj_done")
        s_hT = sem("hT_ready")
        s_t0 = sem("h_turned")
        s_h0 = sem("h0_ready")
        s_st1 = sem("stats1_ready")
        s_mv1 = sem("meanvar1_ready")
        s_r1 = [sem("variance1_plus_eps"), sem("rstd1_ready")]
        s_xn = sem("xn_ready")
        s_t1 = sem("xn_turned")
        s_xnT = sem("xnT_ready")
        s_up = sem("up_done")
        s_ra = sem("relu_by_act")
        s_rd = sem("relu_by_dve")
        s_kq = sem("kq_done")
        s_k = sem("kT_ready")
        s_q = sem("qT_ready")
        s_em = sem("emb_done")
        s_emb = sem("emb_ready")
        s_sc = sem("scores_done")
        s_nm = sem("nmax_ready")
        s_exp = sem("exp_done")
        s_ta = sem("prob_turned")
        s_pa = sem("probT_by_act")
        s_pd = sem("probT_by_dve")
        s_ri = sem("rinv_ready")
        s_o = sem("attention_done")
        s_h1 = sem("h1_ready")
        s_st2 = sem("stats2_ready")
        s_mv2 = sem("meanvar2_ready")
        s_r2 = [sem("variance2_plus_eps"), sem("rstd2_ready")]
        s_xm = sem("xm_ready")
        s_t2 = sem("xm_turned")
        s_xmT = sem("xmT_ready")
        s_l = sem("logits_done")
        s_lg = sem("logits_kept")
        s_out = [sem("rows_stored_0"), sem("rows_stored_1")]
        b_lm = sem("lmax_ready")
        b_lt = sem("lmax_turned")
        b_gm = sem("gmax_steps")
        b_gb = sem("gmax_spread")
        b_ng = sem("ngmax_ready")
        b_ex = sem("p_ready")
        b_su = sem("sum_done")
        b_pi = sem("pinv_ready")
        b_in = sem("search_set")
        b_ca = sem("candidate_ready")
        b_ct = sem("counts_ready")
        b_tt = sem("totals_done")
        b_kp = sem("keep_ready")
        b_th = sem("threshold_ready")
        b_gt = sem("above_ready")
        b_eq = sem("equal_ready")
        b_nd = sem("need_ready")
        b_rk = sem("tie_ranks_done")
        b_sc = sem("scan_steps")
        b_se = sem("sel_ready")
        b_tb = sem("table_done")
        b_ta = sem("table_kept")
        b_pf = sem("first_ranks_done")
        b_fr = sem("first_ranks_kept")
        b_pa = sem("past_ready")
        b_ho = sem("hot_ready")
        b_lo = sem("lookup_done")
        b_sl = sem("slot_ready")
        b_pl = sem("place_ready")
        b_ro = sem("rows_ready")
        c_g = [sem("gathered_0"), sem("gathered_1")]
        c_st = sem("stats3_ready")
        c_mv = sem("meanvar3_ready")
        c_r = [sem("variance3_plus_eps"), sem("rstd3_ready")]
        c_xn = sem("gathered_normalised")
        c_t = sem("gathered_turned")
        c_gT = sem("gT_ready")
        c_v = sem("val_logits_done")
        c_ve = sem("val_exp_done")
        c_va = sem("val_ready")
        c_up = sem("expert_up_done")
        c_ge = sem("gelu_done")
        c_dn = sem("expert_down_done")
        c_yb = sem("y_biased")
        c_y = sem("y_ready")
        c_sc = [sem("rows_added_0"), sem("rows_added_1")]

        NW = 16

        def slot16(t, par):
            return 8 * (t - par) + 16

        def wait(eng, s, value):
            if not isinstance(value, int) or value > 0:
                eng.wait_ge(s, value)

        def steps(eng, step):
            for t in range(-2, 2):
                step(t, t % 2)
            with eng.Fori(2, PAIRS - 3, 2) as i:
                step(i, 0)
                step(i + 1, 1)
            for t in range(PAIRS - 2, PAIRS + 1):
                step(t, t % 2)

        def there(t):
            return not isinstance(t, int) or 0 <= t < PAIRS

        block = ctx.enter_context(nc.Block())

        @block.sync
        def _(sp):
            for dst, src in ((tokw_s, tok_w), (tokb_s, tok_b), (cls_s, cls), (pos_s, pos),
                             (ident_s, ident), (wup_s, w_up), (bup_s, b_up), (we2_s, w_e2),
                             (be2_s, b_e2), (wkq_s, w_kq), (bkq_s, b_kq), (wr_s, wr),
                             (upto_s, upto), (after_s, after), (before_s, before),
                             (number_s, number)):
                sp.dma_start(dst[:], src).then_inc(s_w, 16)

            def load_x(t, par):
                wait(sp, s_proj, t - 1)
                sp.dma_start(xs[:, par], x[t]).then_inc(s_x[par], 16)

            def load_txt(t, par):
                wait(sp, s_h1, t - 1)
                sp.dma_start(h0[IMG_ROWS1:HALF, par, :, 1, :], txt[t]).then_inc(s_txt[par], 16)

            def store(t, par):
                wait(sp, s_h1, t + 1)
                sp.dma_start(pair_rows[t], h1[:, par]).then_inc(s_out[par], 16)

            for t in range(2):
                load_x(t, t)
                load_txt(t, t)
            for dst, src in ((rank_s, rank), (w1_s, w1), (b1_s, b1), (w2_s, w2), (b2_s, b2)):
                sp.dma_start(dst[:], src).then_inc(s_w2, 16)
            for t in range(2):
                load_x(t + 2, t)
                store(t, t)
                load_txt(t + 2, t)
            with sp.Fori(2, PAIRS - 3, 2) as i:
                for par in range(2):
                    load_x(i + par + 2, par)
                    store(i + par, par)
                    load_txt(i + par + 2, par)
            store(PAIRS - 2, 0)
            store(PAIRS - 1, 1)

        @block.tensor
        def _(pe):
            pe.wait_ge(s_w, 16 * NW)
            pe.wait_ge(s_ht0, 1)

            def project(t, par):
                pe.wait_ge(s_x[par], slot16(t, par))
                wait(pe, s_hT, t - 1)
                wait(pe, s_lg, t - 2)
                for k in range(PK):
                    last = pe.matmul(B[par][:, 0:2 * PATCHES], tokw_s[:, k, :], xs[:, par, k, :],
                                     start=(k == 0), stop=(k == PK - 1))
                last.then_inc(s_proj, 1)

            def turn_h(t, par):
                pe.wait_ge(s_hT, t + 1)
                wait(pe, s_k, t)
                wait(pe, s_q, t)
                for m in range(2):
                    pe.transpose(B[6][0:HALF, (2 * m) * D:(2 * m + 1) * D], hT[:, par, m, 0:HALF],
                                 ident_s[:])
                    last = pe.transpose(B[6][0:IMG_ROWS1, (2 * m + 1) * D:(2 * m + 2) * D],
                                        hT[:, par, m, HALF:HALF + IMG_ROWS1], ident_s[:])
                last.then_inc(s_t0, 1)

            def turn_rows(bank, src, done):
                for c in range(4):
                    last = pe.transpose(bank[:, c * HALF:(c + 1) * HALF], src[:, c, :],
                                        ident_s[0:HALF, 0:HALF])
                last.then_inc(done, 1)

            def up(t):
                pe.wait_ge(s_xnT, t + 1)
                for m in range(4):
                    if m == 0:
                        wait(pe, s_pa, t)
                    if m == 1:
                        wait(pe, s_pd, t)
                    if m == 2:
                        pe.wait_ge(s_ra, 2 * t + 1)
                    if m == 3:
                        pe.wait_ge(s_rd, 2 * t + 1)
                    pe.matmul(B[2 + m % 2][:, 0:2 * TOK], wup_s[:, m, :], xnT[:], start=True,
                              stop=True).then_inc(s_up, 1)

            def keys(t):
                pe.wait_ge(s_ra, 2 * t + 1)
                pe.wait_ge(s_rd, 2 * t + 1)
                for m in range(2):
                    last = pe.matmul(B[6][:, 0:2 * TOK], wkq_s[:, m, :], hid[:, m, :],
                                     start=(m == 0), stop=(m == 1))
                last.then_inc(s_kq, 1)

            def embed(t):
                pe.wait_ge(s_ra, 2 * t + 2)
                pe.wait_ge(s_rd, 2 * t + 2)
                wait(pe, s_h1, t)
                for c in range(4):
                    for m in range(2):
                        last = pe.matmul(B[7][0:HALF, c * D:(c + 1) * D],
                                         hid[:, 2 + m, c * HALF:(c + 1) * HALF], we2_s[:, m, :],
                                         start=(m == 0), stop=(m == 1))
                last.then_inc(s_em, 1)

            def scores(t, m):
                if m == 0:
                    pe.wait_ge(s_k, t + 1)
                    pe.wait_ge(s_q, t + 1)
                    wait(pe, s_exp, 2 * t - 1)
                if m == 1:
                    wait(pe, s_xmT, t)
                for c in range(2):
                    at = m * TOK + c * HALF
                    last = pe.matmul(B[4 + m][0:HALF, c * TOK:(c + 1) * TOK],
                                     qT[:, at:at + HALF], kT[:, m * TOK:(m + 1) * TOK],
                                     start=True, stop=True)
                last.then_inc(s_sc, 1)

            def turn_xm(t):
                pe.wait_ge(s_xm, t + 1)
                pe.wait_ge(s_exp, 2 * t + 2)
                turn_rows(B[5], xm, s_t2)

            def logits(t, par):
                pe.wait_ge(s_xmT, t + 1)
                wait(pe, s_hT, t + 2 if not isinstance(t, int) else min(t + 2, PAIRS))
                wait(pe, s_lg, t - 1)
                for c in range(4):
                    last = pe.matmul(B[1 - par][0:HALF, 384 + c * E:384 + (c + 1) * E],
                                     xmT[:, c * HALF:(c + 1) * HALF], wr_s[:], start=True, stop=True)
                last.then_inc(s_l, 1)

            def turn_prob(t):
                for m in range(2):
                    pe.wait_ge(s_exp, 2 * t + 1 + m)
                    for kh in range(2):
                        for qh in range(2):
                            last = pe.transpose(
                                B[2 + m][0:HALF, kh * TOK + qh * HALF:kh * TOK + (qh + 1) * HALF],
                                prob[:, 2 * m + qh, kh * HALF:(kh + 1) * HALF],
                                ident_s[0:HALF, 0:HALF])
                    last.then_inc(s_ta, 1)

            def attend(t):
                pe.wait_ge(s_emb, t + 1)
                for m in range(2):
                    pe.wait_ge(s_pa if m == 0 else s_pd, t + 1)
                    for qh in range(2):
                        c = 2 * m + qh
                        for kh in range(2):
                            last = pe.matmul(B[7][0:HALF, c * D:(c + 1) * D],
                                             probT[:, m, kh, qh * HALF:(qh + 1) * HALF],
                                             emb[:, 2 * m + kh, :], start=(kh == 0), stop=(kh == 1))
                last.then_inc(s_o, 1)

            def step(t, par):
                if there(t):
                    up(t)
                    keys(t)
                    embed(t)
                if there(t - 1):
                    turn_xm(t - 1)
                if there(t):
                    scores(t, 0)
                if there(t - 1):
                    logits(t - 1, 1 - par)
                if there(t):
                    scores(t, 1)
                if there(t + 1):
                    turn_h(t + 1, 1 - par)
                if there(t + 2):
                    project(t + 2, par)
                if there(t):
                    turn_prob(t)
                if there(t + 1):
                    pe.wait_ge(s_xn, t + 2)
                    turn_rows(B[6], xn, s_t1)
                if there(t):
                    attend(t)

            steps(pe, step)

            pe.wait_ge(s_const, 2)
            pe.wait_ge(b_lm, 1)
            pe.transpose(B[0][0:E, 0:HALF], lmax[:], ident_s[0:HALF, 0:HALF]).then_inc(b_lt, 1)
            pe.wait_ge(b_gm, 2)
            pe.matmul(B[1][:, 0:E], ones_s[0:E, :], gdiag[:], start=True, stop=True).then_inc(b_gb, 1)
            pe.wait_ge(b_ex, 1)
            pe.matmul(B[2][:, 0:E], ones_s[0:HALF, :], psum_p[:], start=True, stop=True).then_inc(b_su, 1)
            with pe.Fori(1, BITS + 1) as i:
                pe.wait_ge(b_ct, i)
                pe.matmul(B[0][0:HALF, 0:E], ones_s[0:HALF, 0:HALF], cnt[:], start=True,
                          stop=True).then_inc(b_tt, 1)
            pe.wait_ge(b_ct, BITS + 1)
            pe.matmul(B[0][0:HALF, 0:E], ones_s[0:HALF, 0:HALF], cnt[:], start=True,
                      stop=True).then_inc(b_tt, 1)
            pe.wait_ge(b_eq, 1)
            for e in range(E):
                if e >= 2:
                    pe.wait_ge(b_se, e - 1)
                pe.matmul(B[2 + e % 2][0:HALF, 0:COLS], after_b[:], eq[:, e, :], start=True, stop=True)
                pe.matmul(B[4 + e % 2][0:HALF, 0:COLS], ones_b[:], eq[:, e, :], start=True,
                          stop=True).then_inc(b_rk, 1)
            for e in range(E):
                pe.wait_ge(b_se, e + 1)
                if e >= 2:
                    pe.wait_ge(b_ta, e - 1)
                for b in range(BLK):
                    last = pe.matmul(B[6 + e % 2][:, b * HALF:(b + 1) * HALF],
                                     sel[:, e, b * 128:(b + 1) * 128], upto_b[:], start=True, stop=True)
                last.then_inc(b_tb, 1)
            pe.wait_ge(b_ta, E)
            tot = table[:, :, :, HALF - 1]
            pe.matmul(B[1][:, 0:E], before_s[:], tot[:, :, 0], start=True, stop=True)
            pe.matmul(B[1][:, E:2 * E], before_s[:], tot[:, :, 1], start=True, stop=False)
            pe.matmul(B[1][:, E:2 * E], ones_s[:], tot[:, :, 0], start=False, stop=True).then_inc(b_pf, 1)
            for e in range(E):
                pe.wait_ge(b_ho, e + 1)
                if e >= 2:
                    pe.wait_ge(b_ro, e - 1)
                for c in range(CH):
                    at = 2 + 2 * (e % 2) + c // 4
                    for b in range(BLK):
                        last = pe.matmul(B[at][:, (c % 4) * 96:(c % 4) * 96 + TW],
                                         hot[:, e % 2, b, c * 128:(c + 1) * 128], table[:, e, b, :],
                                         start=(b == 0), stop=(b == BLK - 1))
                last.then_inc(b_lo, 1)

            for e in range(E):
                pe.wait_ge(c_xn, e + 1)
                for q in range(2):
                    if e >= 1:
                        pe.wait_ge(c_gT, 2 * e - 1 + q)
                    for c in range(4):
                        last = pe.transpose(B[6 + q][:, c * 128:(c + 1) * 128], g[:, e * CH + 4 * q + c, :],
                                            ident_s[:])
                    last.then_inc(c_t, 1)
                pe.wait_ge(c_gT, 2 * e + 2)
                for c in range(CH):
                    last = pe.matmul(B[0][:, e * CH + c:e * CH + c + 1], gT[:, e * CH + c, :],
                                     wr_s[:, e:e + 1], start=True, stop=True)
            last.then_inc(c_v, 1)
            pe.wait_ge(s_w2, 16 * 5)
            for n in range(2 * E + 1):
                if n < 2 * E:
                    e = n // 2
                    for f in range(FT):
                        k = n * FT + f
                        if k >= 4:
                            pe.wait_ge(c_ge, k - 3)
                        pe.matmul(B[2 + k % 4][:, :], w1_s[:, e, f * 128:(f + 1) * 128],
                                  gT[:, 4 * n:4 * n + 4, :], start=True, stop=True).then_inc(c_up, 1)
                if n >= 1:
                    o = n - 1
                    e = o // 2
                    pe.wait_ge(c_ge, FT * (o + 1))
                    if o >= 2:
                        pe.wait_ge(c_yb, o - 1)
                    for c in range(4):
                        for f in range(FT):
                            last = pe.matmul(B[6 + o % 2][:, c * D:(c + 1) * D],
                                             act1[:, o % 2, f, c * 128:(c + 1) * 128], w2_s[:, e, f, :],
                                             start=(f == 0), stop=(f == FT - 1))
                    last.then_inc(c_dn, 1)

        @block.scalar
        def _(act):
            act.wait_ge(s_w, 16 * NW)
            for par in range(2):
                for m in range(2):
                    last = act.copy(hT[:, par, m, 0:1], cls_s[:])
            last.then_inc(s_ht0, 1)

            def keep_hT(t, par):
                act.wait_ge(s_proj, t + 1)
                wait(act, s_t0, t - 1)
                act.activation(hT[:, par, :, 1:1 + PATCHES],
                               B[par][:, 0:2 * PATCHES].rearrange("p (m n) -> p m n", m=2),
                               ACT.Identity, bias=tokb_s[:]).then_inc(s_hT, 1)

            def relus(t):
                for m in range(0, 4, 2):
                    act.wait_ge(s_up, 4 * t + 1 + m)
                    wait(act, s_kq if m == 0 else s_em, t)
                    act.activation(hid[:, m, :], B[2][:, 0:2 * TOK], ACT.Relu,
                                   bias=bup_s[:, m:m + 1]).then_inc(s_ra, 1)

            def keep_k(t):
                act.wait_ge(s_kq, t + 1)
                wait(act, s_sc, 2 * t)
                act.activation(kT[:], B[6][0:DA, 0:2 * TOK], ACT.Identity,
                               bias=bkq_s[0:DA, :]).then_inc(s_k, 1)

            def keep_xmT(t):
                act.wait_ge(s_t2, t + 1)
                wait(act, s_l, t)
                act.copy(xmT[:], B[5][:, 0:2 * TOK]).then_inc(s_xmT, 1)

            def exps(t):
                for m in range(2):
                    act.wait_ge(s_nm, 2 * t + 1 + m)
                    if m == 0:
                        wait(act, s_ta, 2 * t)
                        wait(act, s_ri, t)
                    for c in range(2):
                        k = 2 * m + c
                        last = act.activation(prob[:, k, :], B[4 + m][0:HALF, c * TOK:(c + 1) * TOK],
                                              ACT.Exp, bias=nmax[:, k:k + 1],
                                              accum_out=rsum[:, k:k + 1])
                    last.then_inc(s_exp, 1)

            def keep_probT(t):
                act.wait_ge(s_ta, 2 * t + 1)
                wait(act, s_o, t)
                act.copy(probT[:, 0, :, :], B[2][0:HALF, 0:2 * TOK].rearrange("p (k q) -> p k q", k=2)
                         ).then_inc(s_pa, 1)

            def keep_xnT(t):
                act.wait_ge(s_t1, t + 1)
                wait(act, s_up, 4 * t)
                act.copy(xnT[:], B[6][:, 0:2 * TOK]).then_inc(s_xnT, 1)

            def step(t, par):
                if there(t):
                    relus(t)
                    keep_k(t)
                if there(t - 1):
                    keep_xmT(t - 1)
                if there(t):
                    exps(t)
                if there(t + 2):
                    keep_hT(t + 2, par)
                if there(t):
                    keep_probT(t)
                if there(t + 1):
                    keep_xnT(t + 1)

            steps(act, step)

            act.wait_ge(b_ng, 1)
            for e in range(E):
                last = act.activation(pe_[:, e, :], lg[:, e, :], ACT.Exp, bias=ngmax[0:HALF, e:e + 1],
                                      accum_out=psum_p[:, e:e + 1])
            last.then_inc(b_ex, 1)
            for e in range(E):
                for q in range(2):
                    act.wait_ge(c_t, 2 * e + q + 1)
                    act.copy(gT[:, e * CH + 4 * q:e * CH + 4 * q + 4, :],
                             B[6 + q][:].rearrange("p (c n) -> p c n", c=4)).then_inc(c_gT, 1)
            act.wait_ge(c_v, 1)
            for e in range(E):
                last = act.activation(val[:, e, :], B[0][:, e * CH:(e + 1) * CH], ACT.Exp,
                                      bias=ngmax[:, e:e + 1])
            last.then_inc(c_ve, 1)
            act.wait_ge(s_w2, 16 * 5)
            for n in range(2 * E):
                if n >= 2:
                    act.wait_ge(c_dn, n - 1)
                for f in range(FT):
                    k = n * FT + f
                    act.wait_ge(c_up, k + 1)
                    act.activation(act1[:, n % 2, f, :], B[2 + k % 4][:, :], ACT.Gelu,
                                   bias=b1_s[:, n // 2, f:f + 1]).then_inc(c_ge, 1)

        @block.vector
        def _(dve):
            dve.memset(ones_s[:], 1.0)
            dve.memset(ones_b[:], 1.0)
            dve.memset(half_s[:], -0.5)
            dve.memset(eps_s[:], EPS)
            dve.memset(zero_s[:], 0.0).then_inc(s_const, 1)
            dve.wait_ge(s_w, 16 * NW)
            dve.tensor_copy(upto_b[:], upto_s[:])
            dve.tensor_copy(after_b[:], after_s[:]).then_inc(s_const, 1)

            def relus(t):
                for m in range(1, 4, 2):
                    dve.wait_ge(s_up, 4 * t + 1 + m)
                    wait(dve, s_kq if m == 1 else s_em, t)
                    dve.tensor_scalar(hid[:, m, :], B[3][:, 0:2 * TOK], bup_s[:, m:m + 1], 0.0,
                                      ALU.add, ALU.max).then_inc(s_rd, 1)

            def keep_q(t):
                dve.wait_ge(s_kq, t + 1)
                wait(dve, s_sc, 2 * t)
                dve.tensor_scalar(qT[:], B[6][DA:2 * DA, 0:2 * TOK], bkq_s[DA:2 * DA, :], None,
                                  ALU.add).then_inc(s_q, 1)

            def keep_emb(t):
                dve.wait_ge(s_em, t + 1)
                dve.tensor_tensor(emb[:], B[7][0:HALF, :].rearrange("p (c d) -> p c d", c=4),
                                  be2_s[0:HALF, :].unsqueeze(1).to_broadcast([HALF, 4, D]),
                                  ALU.add).then_inc(s_emb, 1)

            def maxima(t, m):
                dve.wait_ge(s_sc, 2 * t + 1 + m)
                wait(dve, s_exp, 2 * t)
                dve.tensor_reduce(nmax[:, 2 * m:2 * m + 2],
                                  B[4 + m][0:HALF, 0:2 * TOK].rearrange("p (c k) -> p c k", c=2),
                                  AX.X, ALU.max, negate=True).then_inc(s_nm, 1)

            def keep_logits(t, par):
                dve.wait_ge(s_l, t + 1)
                dve.tensor_copy(lg[:, :, bass.ds(4 * t, 4)].rearrange("p e c -> p c e"),
                                B[1 - par][0:HALF, 384:384 + 4 * E].rearrange("p (c e) -> p c e", c=4)
                                ).then_inc(s_lg, 1)

            def stats(t, rows, st, mv, ready, s_st, s_mv, used):
                wait(dve, used, t)
                for c in range(4):
                    last = dve.bn_stats(st[:, c, :], rows[:, c, :])
                last.then_inc(s_st, 1)
                dve.wait_ge(s_const, 1)
                dve.wait_ge(s_st, t + 1)
                for c in range(4):
                    last = dve.bn_aggr(mv[:, c, :], st[:, c, :])
                last.then_inc(s_mv, 1)

            def keep_h0(t, par):
                dve.wait_ge(s_t0, t + 1)
                turned = B[6][:, :].rearrange("p (m c d) -> p m c d", m=2, c=2)
                dve.tensor_scalar(h0[:, par, :, 0, :], turned[0:HALF, :, 0, :], pos_s[:, 0:1], None,
                                  ALU.add)
                dve.tensor_scalar(h0[0:IMG_ROWS1, par, :, 1, :], turned[0:IMG_ROWS1, :, 1, :],
                                  pos_s[0:IMG_ROWS1, 1:2], None, ALU.add).then_inc(s_h0, 1)
                dve.wait_ge(s_h0, t + 1)
                dve.wait_ge(s_txt[par], slot16(t, par))
                stats(t, h0[:, par].rearrange("p m c d -> p (m c) d"), st1, mv1, s_h0, s_st1, s_mv1,
                      s_xn)

            def keep_probT(t):
                dve.wait_ge(s_ta, 2 * t + 2)
                wait(dve, s_o, t)
                dve.tensor_copy(probT[:, 1, :, :],
                                B[3][0:HALF, 0:2 * TOK].rearrange("p (k q) -> p k q", k=2)
                                ).then_inc(s_pd, 1)
                dve.reciprocal(rinv[:], rsum[:]).then_inc(s_ri, 1)

            def residual(t, par):
                dve.wait_ge(s_o, t + 1)
                dve.wait_ge(s_ri, t + 1)
                wait(dve, s_out[par], slot16(t - 2, par))
                wait(dve, s_xm, t - 1)
                for c in range(4):
                    last = dve.scalar_tensor_tensor(out=h1[:, par, c, :], in0=B[7][0:HALF, c * D:(c + 1) * D],
                                                    scalar=rinv[:, c:c + 1], in1=h0[:, par, c // 2, c % 2, :],
                                                    op0=ALU.mult, op1=ALU.add)
                last.then_inc(s_h1, 1)
                dve.wait_ge(s_h1, t + 1)
                stats(t, h1[:, par], st2, mv2, s_h1, s_st2, s_mv2, s_xm)

            def step(t, par):
                if there(t):
                    relus(t)
                    keep_q(t)
                    keep_emb(t)
                    maxima(t, 0)
                if there(t - 1):
                    keep_logits(t - 1, 1 - par)
                if there(t):
                    maxima(t, 1)
                if there(t + 1):
                    keep_h0(t + 1, 1 - par)
                if there(t):
                    keep_probT(t)
                    residual(t, par)

            steps(dve, step)

            dve.wait_ge(s_lg, PAIRS)
            dve.tensor_reduce(lmax[:], lg[:], AX.X, ALU.max).then_inc(b_lm, 1)
            dve.wait_ge(b_lt, 1)
            dve.tensor_reduce(gmax[:], B[0][0:E, 0:HALF], AX.X, ALU.max).then_inc(b_gm, 1)
            dve.wait_ge(b_gm, 1)
            dve.tensor_scalar(gdiag[:], ident_s[0:E, 0:E], gmax[:], -1.0, ALU.mult, ALU.mult).then_inc(b_gm, 1)
            dve.wait_ge(b_gb, 1)
            dve.tensor_copy(ngmax[:], B[1][:, 0:E]).then_inc(b_ng, 1)
            dve.memset(thr[:], 0)
            dve.memset(cand[:], TOP_BIT)
            dve.memset(bit[:], TOP_BIT).then_inc(b_in, 1)
            dve.wait_ge(b_in, 1)
            dve.wait_ge(b_su, 1)
            dve.reciprocal(pinv[:], B[2][:, 0:E]).then_inc(b_pi, 1)

            with dve.Fori(1, BITS + 1) as i:
                for e in range(E):
                    last = dve.tensor_scalar(gt[:, e, :], pe_[:, e, :], cand[:, e:e + 1].bitcast(f32),
                                             None, ALU.is_ge, ALU.add, accum_out=cnt[:, e:e + 1])
                last.then_inc(b_ct, 1)
                dve.tensor_scalar(bit[:], bit[:], 1, None, ALU.logical_shift_right).then_inc(b_in, 1)
                dve.wait_ge(b_tt, i)
                dve.tensor_scalar(keep[:], B[0][0:HALF, 0:E], float(CAP), None, ALU.is_ge).then_inc(b_kp, 1)
                dve.wait_ge(s_const, 1)
                dve.wait_ge(b_kp, i)
                dve.copy_predicated(thr[:], keep[:], cand[:]).then_inc(b_th, 1)
                dve.wait_ge(b_th, i)
                dve.wait_ge(b_in, i + 1)
                dve.tensor_tensor(cand[:], thr[:], bit[:].to_broadcast([HALF, E]), ALU.bitwise_or
                                  ).then_inc(b_ca, 1)
                dve.wait_ge(b_ca, i)

            limit = thr[:].bitcast(f32)
            for e in range(E):
                last = dve.tensor_scalar(gt[:, e, :], pe_[:, e, :], limit[:, e:e + 1], None, ALU.is_gt,
                                         ALU.add, accum_out=cnt[:, e:e + 1])
            last.then_inc(b_ct, 1)
            for e in range(E):
                last = dve.tensor_scalar(eq[:, e, :], pe_[:, e, :], limit[:, e:e + 1], None, ALU.is_equal)
            last.then_inc(b_eq, 1)
            dve.wait_ge(b_tt, BITS + 1)
            dve.tensor_scalar(need[:], B[0][0:HALF, 0:E], -1.0, float(CAP), ALU.mult, ALU.add).then_inc(b_nd, 1)
            dve.wait_ge(b_nd, 1)
            dve.wait_ge(b_eq, 1)
            for e in range(E):
                k = e % 2
                dve.wait_ge(b_rk, e + 1)
                dve.tensor_tensor_scan(scan[:, k, :], zero_s[:], B[4 + k][0:HALF, 0:COLS], 0.0, ALU.add,
                                       ALU.add).then_inc(b_sc, 1)
                dve.wait_ge(b_sc, 3 * e + 1)
                dve.tensor_tensor(rk[:, k, :], scan[:, k, :], B[2 + k][0:HALF, 0:COLS], ALU.add).then_inc(b_sc, 1)
                dve.wait_ge(b_sc, 3 * e + 2)
                dve.scalar_tensor_tensor(out=tie[:, k, :], in0=rk[:, k, :], scalar=need[:, e:e + 1],
                                         in1=eq[:, e, :], op0=ALU.is_le, op1=ALU.mult).then_inc(b_sc, 1)
                dve.wait_ge(b_sc, 3 * e + 3)
                dve.tensor_tensor(sel[:, e, :], tie[:, k, :], gt[:, e, :], ALU.add).then_inc(b_se, 1)
            for e in range(E):
                dve.wait_ge(b_tb, e + 1)
                dve.tensor_copy(table[:, e, :, 0:HALF],
                                B[6 + e % 2][:, 0:BLK * HALF].rearrange("p (b n) -> p b n", b=BLK)
                                ).then_inc(b_ta, 1)
            dve.wait_ge(b_pf, 1)
            first = B[1][:, 0:2 * E].rearrange("p (b e) -> p e b", b=BLK)
            dve.tensor_copy(table[:, :, :, HALF], first)
            dve.tensor_copy(table[:, :, :, HALF + 1],
                            number_s[:, CH:CH + BLK].unsqueeze(1).to_broadcast([128, E, BLK]))
            dve.tensor_tensor(incl[:], table[:, :, :, HALF - 1], first, ALU.add).then_inc(b_fr, 1)
            dve.wait_ge(b_fr, 1)
            dve.wait_ge(s_w2, 16 * 5)

            def hots(e):
                k = e % 2
                if e >= 1:
                    dve.wait_ge(b_ho, e)
                if e >= 2:
                    dve.wait_ge(b_lo, e - 1)
                for b in range(BLK):
                    last = dve.tensor_scalar(past[:, b, :], rank_s[:], incl[:, e, b:b + 1], None, ALU.is_ge)
                last.then_inc(b_pa, 1)
                dve.wait_ge(b_pa, e + 1)
                for b in range(BLK):
                    last = dve.scalar_tensor_tensor(out=hot[:, k, b, :], in0=rank_s[:],
                                                    scalar=table[:, e, b, HALF:HALF + 1], in1=past[:, b, :],
                                                    op0=ALU.is_ge, op1=ALU.subtract)
                last.then_inc(b_ho, 1)

            def find_rows(e):
                k = e % 2
                dve.wait_ge(b_lo, e + 1)
                for q in range(2):
                    looked = B[2 + 2 * k + q][:, 0:384].rearrange("p (c n) -> p c n", c=4)
                    last = dve.tensor_tensor(slot[:, k, 4 * q:4 * q + 4], number_s[:, 4 * q:4 * q + 4],
                                             looked[:, :, HALF], ALU.subtract)
                last.then_inc(b_sl, 1)
                dve.wait_ge(b_sl, e + 1)
                for c in range(CH):
                    at = (c % 4) * 96
                    last = dve.tensor_scalar(passed[:, c, :], B[2 + 2 * k + c // 4][:, at:at + HALF],
                                             slot[:, k, c:c + 1], None, ALU.is_le, ALU.add,
                                             accum_out=place[:, k, c:c + 1])
                last.then_inc(b_pl, 1)
                dve.wait_ge(b_pl, e + 1)
                for q in range(2):
                    looked = B[2 + 2 * k + q][:, 0:384].rearrange("p (c n) -> p c n", c=4)
                    last = dve.scalar_tensor_tensor(out=row[:, e, 4 * q:4 * q + 4],
                                                    in0=looked[:, :, HALF + 1], scalar=float(HALF),
                                                    in1=place[:, k, 4 * q:4 * q + 4], op0=ALU.mult, op1=ALU.add)
                last.then_inc(b_ro, 1)

            def gathered_stats(e):
                k = e % 2
                dve.wait_ge(c_g[k], 16 * CH * (e // 2 + 1))
                if e >= 2:
                    dve.wait_ge(c_xn, e - 1)
                for c in range(CH):
                    last = dve.bn_stats(st3[:, k, c, :], g[:, e * CH + c, :])
                last.then_inc(c_st, 1)
                dve.wait_ge(c_st, e + 1)
                for c in range(CH):
                    last = dve.bn_aggr(mv3[:, k, c, :], st3[:, k, c, :])
                last.then_inc(c_mv, 1)

            for e in range(E + 2):
                if e < E:
                    hots(e)
                if 1 <= e <= E:
                    find_rows(e - 1)
                if e >= 2:
                    gathered_stats(e - 2)

            dve.wait_ge(c_ve, 1)
            dve.wait_ge(b_pi, 1)
            dve.tensor_tensor(val[:], val[:], pinv[:].unsqueeze(2).to_broadcast([128, E, CH]),
                              ALU.mult).then_inc(c_va, 1)
            dve.wait_ge(c_va, 1)
            for n in range(2 * E):
                e, q = n // 2, n % 2
                dve.wait_ge(c_dn, n + 1)
                if n >= 4:
                    dve.wait_ge(c_sc[e % 2], 16 * CH * (e // 2))
                dve.tensor_tensor(y[:, n % 4], B[6 + n % 2][:].rearrange("p (c d) -> p c d", c=4),
                                  b2_s[:, e, :].unsqueeze(1).to_broadcast([128, 4, D]),
                                  ALU.add).then_inc(c_yb, 1)
                dve.wait_ge(c_yb, n + 1)
                dve.tensor_tensor(y[:, n % 4], y[:, n % 4],
                                  val[:, e, 4 * q:4 * q + 4].unsqueeze(2).to_broadcast([128, 4, D]),
                                  ALU.mult).then_inc(c_y, 1)

        @block.gpsimd
        def _(pool):
            pool.wait_ge(s_const, 1)

            def normalise(t, n, rows, mv, rs, outs, s_r, done):
                pool.tensor_tensor(rs[:, 0, :], mv[:, :, 1], eps_s[0:rs.shape[0], 0:n], ALU.add).then_inc(s_r[0], 1)
                pool.wait_ge(s_r[0], t + 1)
                pool.tensor_tensor(rs[:, 1, :], rs[:, 0, :], half_s[0:rs.shape[0], 0:n], ALU.pow).then_inc(s_r[1], 1)
                pool.wait_ge(s_ht0, 1)
                pool.wait_ge(s_r[1], t + 1)
                for c in range(n):
                    last = pool.tensor_scalar(outs[:, c, :], rows[:, c, :], mv[:, c, 0:1],
                                              rs[:, 1, c:c + 1], ALU.subtract, ALU.mult)
                last.then_inc(done, 1)

            def step(t, par):
                if there(t - 1):
                    pool.wait_ge(s_mv2, t)
                    wait(pool, s_t2, t - 1)
                    normalise(t - 1, 4, h1[:, 1 - par], mv2, rs2, xm, s_r2, s_xm)
                if there(t + 1):
                    pool.wait_ge(s_mv1, t + 2)
                    wait(pool, s_t1, t + 1)
                    normalise(t + 1, 4, h0[:, 1 - par].rearrange("p m c d -> p (m c) d"), mv1, rs1, xn,
                              s_r1, s_xn)

            steps(pool, step)

            for par in range(2):
                pool.wait_ge(s_out[par], 16 * (PAIRS // 2))
            for e in range(E + 1):
                if e < E:
                    pool.wait_ge(b_ro, e + 1)
                    for c in range(CH):
                        pool.indirect_dma_start(out=g[:, e * CH + c, :], out_offset=None, in_=rows_dram,
                                                in_offset=bass.IndirectOffsetOnAxis(ap=row[:, e, c:c + 1], axis=0)
                                                ).then_inc(c_g[e % 2], 16)
                if e >= 1:
                    o = e - 1
                    rows = g[:, o * CH:(o + 1) * CH, :]
                    pool.wait_ge(c_mv, o + 1)
                    normalise(o, CH, rows, mv3[:, o % 2], rs3[:, o % 2], rows, c_r, c_xn)
            for k in range(2):
                pool.wait_ge(c_g[k], 16 * CH * (E // 2))
            for n in range(2 * E):
                e, q = n // 2, n % 2
                pool.wait_ge(c_y, n + 1)
                if q == 0 and e >= 1:
                    pool.wait_ge(c_sc[(e - 1) % 2], 16 * CH * ((e - 1) // 2 + 1))
                for c in range(4):
                    pool.indirect_dma_start(out=rows_dram, in_=y[:, n % 4, c, :], in_offset=None,
                                            out_offset=bass.IndirectOffsetOnAxis(
                                                ap=row[:, e, 4 * q + c:4 * q + c + 1], axis=0),
                                            compute_op=ALU.add).then_inc(c_sc[e % 2], 16)
            for k in range(2):
                pool.wait_ge(c_sc[k], 16 * CH * (E // 2))


def kernel(x, txt, L0_tok_W, L0_tok_b, L0_tok_cls_token, L0_tok_pos_emb, L0_attn_We1, L0_attn_be1,
           L0_attn_We2, L0_attn_be2, L0_attn_Wk1, L0_attn_bk1, L0_attn_Wk2, L0_attn_bk2, L0_ffn_Wr,
           L0_ffn_W1, L0_ffn_b1, L0_ffn_W2, L0_ffn_b2):
    import numpy as np
    import concourse.bacc as bacc
    from concourse.bass_utils import run_bass_kernel_spmd

    def a(v):
        return np.asarray(v)

    def tiles(v, n):
        return v.reshape((n, 128) + v.shape[1:]).swapaxes(0, 1)

    p = a(x).reshape(PAIRS, 2, 3, 11, 16, 13, 16).transpose(0, 4, 6, 2, 1, 3, 5)
    p = p.reshape(PAIRS, PK, 128, 2 * PATCHES).transpose(0, 2, 1, 3)
    pos = a(L0_tok_pos_emb).reshape(1 + PATCHES)
    pos2 = np.zeros((HALF, 2), pos.dtype)
    pos2[:, 0] = pos[:HALF]
    pos2[:IMG_ROWS1, 1] = pos[HALF:]
    w_up = np.concatenate([a(L0_attn_Wk1), a(L0_attn_We1)], 1).reshape(D, 4, 128)
    b_up = np.concatenate([a(L0_attn_bk1), a(L0_attn_be1)]).reshape(4, 128).T
    n = np.arange(128)
    ins = {
        "x": p,
        "txt": a(txt).reshape(PAIRS, 2, TXT, D).transpose(0, 2, 1, 3),
        "tok_w": tiles(a(L0_tok_W).T, PK),
        "tok_b": a(L0_tok_b).reshape(D, 1),
        "cls": a(L0_tok_cls_token).reshape(D, 1),
        "pos": pos2,
        "w_up": w_up,
        "b_up": b_up,
        "w_e2": tiles(a(L0_attn_We2), 2),
        "b_e2": np.broadcast_to(a(L0_attn_be2), (128, D)),
        "w_kq": tiles(a(L0_attn_Wk2), 2),
        "b_kq": a(L0_attn_bk2).reshape(128, 1),
        "wr": a(L0_ffn_Wr),
        "w1": a(L0_ffn_W1).transpose(1, 0, 2),
        "b1": a(L0_ffn_b1).reshape(E, FT, 128).transpose(2, 0, 1),
        "w2": a(L0_ffn_W2).reshape(E, FT, 128, D).transpose(2, 0, 1, 3),
        "b2": np.broadcast_to(a(L0_ffn_b2), (128, E, D)),
        "ident": np.eye(128, dtype=np.float32),
        "upto": (n[:HALF, None] <= n[None, :HALF]).astype(np.float32),
        "after": -(n[:HALF, None] > n[None, :HALF]).astype(np.float32),
        "before": (n[:, None] < n[None, :]).astype(np.float32),
        "rank": np.broadcast_to(np.arange(CAP, dtype=np.float32), (128, CAP)),
        "number": np.concatenate([n[:, None] + 128 * np.arange(CH)[None, :],
                                  n[:, None] + 128 * np.arange(BLK)[None, :]], 1).astype(np.float32),
    }
    ins = {"in_" + k: np.ascontiguousarray(v) for k, v in ins.items()}
    nc = bacc.Bacc("TRN2", target_bir_lowering=False, num_devices=1)
    args = [nc.dram_tensor(k, v.shape, mybir.dt.from_np(v.dtype), kind="ExternalInput").ap()
            for k, v in ins.items()]
    out = nc.dram_tensor("out", (IMGS, TOK, D), mybir.dt.float32, kind="ExternalOutput").ap()
    fusion_program(nc, *args, out)
    r = run_bass_kernel_spmd(nc, [ins], core_ids=[0])
    return r.results[0]["out"]
```

```python
import concourse.bass as bass
from concourse import mybir
from contextlib import ExitStack

IMGS = 128
PATCHES = 143
TXT = 32
TOK = 1 + PATCHES + TXT
HALF = TOK // 2
D = 128
PK = 6
PAIRS = IMGS // 2
IMG_ROWS1 = 1 + PATCHES - HALF
HID = 256
DA = 64
E = 8
F = 512
FT = F // 128
CAP = 1024
CH = CAP // 128
COLS = 2 * IMGS
BLK = COLS // 128
EPS = 1e-5
GRP = 128 // E
GN = HALF * COLS // GRP
HI_BITS = 14
LO_BITS = 16
TW = HALF + 2


def fusion_program(nc, x, txt, tok_w, tok_b, cls, pos, w_up, b_up, w_e2, b_e2, w_kq, b_kq,
                   wr, w1, b1, w2, b2, ident, upto, after, before, group, rank, number, out):
    f32, bf16, i32, u16 = mybir.dt.float32, mybir.dt.bfloat16, mybir.dt.int32, mybir.dt.uint16
    ALU = mybir.AluOpType
    ACT = mybir.ActivationFunctionType
    AX = mybir.AxisListType

    pair_rows = out.rearrange("(t m) (c p) d -> t p (m c) d", m=2, c=2)
    rows_dram = out.rearrange("i n d -> (i n) d")
    xm_dram = nc.dram_tensor("xm_dram", (IMGS * TOK, D), mybir.dt.float32, kind="Internal").ap()
    xm_pairs = xm_dram.rearrange("(t c p) d -> t p c d", c=4, p=HALF)
    lg_dram = nc.dram_tensor("lg_dram", (E, HALF * COLS), mybir.dt.float32, kind="Internal").ap()

    ctx = ExitStack()
    with ctx:
        def sb(name, shape, dt=f32):
            return ctx.enter_context(nc.sbuf_tensor(name, shape, dt))

        def sem(name):
            return ctx.enter_context(nc.semaphore(name))

        ident_s = sb("ident_s", [128, 128])
        upto_s = sb("upto_s", [HALF, HALF])
        after_s = sb("after_s", [HALF, HALF])
        before_s = sb("before_s", [128, 128])
        group_s = sb("group_s", [128, 128])
        rank_u = sb("rank_u", [128, CAP], u16)
        number_s = sb("number_s", [128, CH + BLK])
        upto_b = sb("upto_b", [HALF, HALF], bf16)
        after_b = sb("after_b", [HALF, HALF], bf16)
        ones_b = sb("ones_b", [HALF, HALF], bf16)
        ones_s = sb("ones_s", [128, 128])
        eps_s = sb("eps_s", [128, 8])
        half_s = sb("half_s", [128, 8])
        tokw_s = sb("tokw_s", [128, PK, D])
        tokb_s = sb("tokb_s", [D, 1])
        cls_s = sb("cls_s", [D, 1])
        pos_s = sb("pos_s", [HALF, 2])
        wup_s = sb("wup_s", [D, 4, 128])
        bup_s = sb("bup_s", [128, 4])
        we2_s = sb("we2_s", [128, 2, D])
        be2_s = sb("be2_s", [128, D])
        wkq_s = sb("wkq_s", [128, 2, 128])
        bkq_s = sb("bkq_s", [128, 1])
        wr_s = sb("wr_s", [D, E])
        w1_s = sb("w1_s", [D, E, F])
        b1_s = sb("b1_s", [128, E, FT])
        w2_s = sb("w2_s", [128, E, FT, D])
        b2_s = sb("b2_s", [128, E, D])

        xs = sb("xs", [128, 2, PK, 2 * PATCHES])
        hT = sb("hT", [D, 2, 2, TOK])
        h0 = sb("h0", [HALF, 2, 2, 2, D])
        st1 = sb("st1", [HALF, 4, 6])
        mv1 = sb("mv1", [HALF, 4, 2])
        rs1 = sb("rs1", [HALF, 2, 4])
        xn = sb("xn", [HALF, 4, D])
        xnT = sb("xnT", [D, 2 * TOK])
        hid = sb("hid", [128, 4, 2 * TOK])
        kT = sb("kT", [DA, 2 * TOK])
        qT = sb("qT", [DA, 2 * TOK])
        emb = sb("emb", [HALF, 4, D])
        nmax = sb("nmax", [HALF, 4])
        rsum = sb("rsum", [HALF, 4])
        rinv = sb("rinv", [HALF, 4])
        prob = sb("prob", [HALF, 4, TOK])
        probT = sb("probT", [HALF, 2, 2, TOK])
        h1 = sb("h1", [HALF, 2, 4, D])
        st2 = sb("st2", [HALF, 4, 6])
        mv2 = sb("mv2", [HALF, 4, 2])
        rs2 = sb("rs2", [HALF, 2, 4])
        xm = sb("xm", [HALF, 2, 4, D])
        xmT = sb("xmT", [D, 2 * TOK])
        lg_y = sb("lg_y", [128, E * COLS])
        lg = lg_y[0:HALF, :].rearrange("p (e c) -> p e c", e=E)

        prb = sb("prb", [HALF, E, COLS])
        lgs = sb("lgs", [128, GN])
        prs = sb("prs", [128, GN])
        hi = sb("hi", [128, GN], u16)
        lo = sb("lo", [128, GN], u16)
        above = sb("above", [128, GN], u16)
        reach = sb("reach", [128, GN], bf16)
        pmax = sb("pmax", [128, 1])
        spread = sb("spread", [128, 128])
        ngmax = sb("ngmax", [128, E])
        ngown = sb("ngown", [128, 1])
        sum_p = sb("sum_p", [HALF, E])
        pinv = sb("pinv", [128, E])
        thr = sb("thr", [128, 2])
        thr_i = sb("thr_i", [128, 2], i32)
        thr_b = sb("thr_b", [128, 1], i32)
        limit = sb("limit", [HALF, E])
        cand = sb("cand", [128, 1])
        bit = sb("bit", [128, 1])
        nbit = sb("nbit", [128, 1])
        kbit = sb("kbit", [128, 1])
        cnt = sb("cnt", [128, 1])
        cntg = sb("cntg", [HALF, E])
        shared = sb("shared", [128, 2 * FT * 512])
        scan = shared[0:HALF, 0:E * COLS].rearrange("p (e c) -> p e c", e=E)
        gteq = shared[0:HALF, E * COLS:2 * E * COLS].bitcast(bf16).rearrange("p (w e c) -> p w e c", w=2, e=E)
        gt, eq = gteq[:, 0], gteq[:, 1]
        need = sb("need", [HALF, E])
        zero_s = sb("zero_s", [HALF, COLS])
        rk = prb
        tie = sb("tie", [HALF, E, COLS], bf16)
        sel = sb("sel", [HALF, E, COLS + 1], bf16)
        dsel = sb("dsel", [HALF, E, COLS], bf16)
        table = sb("table", [128, E, BLK, TW], bf16)
        tot = sb("tot", [128, BLK, E])
        first = sb("first", [128, BLK, E])
        begun = sb("begun", [128, 2, BLK, CAP], bf16)
        passed = sb("passed", [128, CH, HALF], bf16)
        slot = sb("slot", [128, 2, CH])
        place = sb("place", [128, 2, CH])
        row = sb("row", [128, E, CH], i32)

        g = sb("g", [128, 3, CH, D])
        gT = sb("gT", [D, 2, CH, 128])
        vexp = sb("vexp", [128, E, CH])
        val = sb("val", [128, E, CH])
        act1 = shared[:, :].rearrange("p (k f n) -> p k f n", k=2, f=FT)
        y = lg_y[:, :].rearrange("p (k c d) -> p k c d", k=4, c=4)

        B = [ctx.enter_context(nc.psum_tensor(f"bank{n}", [128, 512], f32)) for n in range(8)]

        s_w = sem("weights_loaded")
        s_w2 = sem("late_weights_loaded")
        s_const = sem("constants_made")
        s_ht0 = sem("class_column_set")
        s_x = [sem("x_loaded_0"), sem("x_loaded_1")]
        s_txt = [sem("txt_loaded_0"), sem("txt_loaded_1")]
        s_proj = sem("proj_done")
        s_hT = sem("hT_ready")
        s_t0 = sem("h_turned")
        s_h0 = sem("h0_ready")
        s_st1 = sem("stats1_ready")
        s_mv1 = sem("meanvar1_ready")
        s_r1 = [sem("variance1_plus_eps"), sem("rstd1_ready")]
        s_xn = sem("xn_ready")
        s_t1 = sem("xn_turned")
        s_xnT = sem("xnT_ready")
        s_up = sem("up_done")
        s_ra = sem("relu_by_act")
        s_rd = sem("relu_by_dve")
        s_kq = sem("kq_done")
        s_k = sem("kT_ready")
        s_q = sem("qT_ready")
        s_em = sem("emb_done")
        s_emb = sem("emb_ready")
        s_sc = sem("scores_done")
        s_nm = sem("nmax_ready")
        s_exp = sem("exp_done")
        s_ta = sem("prob_turned")
        s_pa = sem("probT_by_act")
        s_pd = sem("probT_by_dve")
        s_ri = sem("rinv_ready")
        s_o = sem("attention_done")
        s_h1 = sem("h1_ready")
        s_st2 = sem("stats2_ready")
        s_mv2 = sem("meanvar2_ready")
        s_r2 = [sem("variance2_plus_eps"), sem("rstd2_ready")]
        s_xm = sem("xm_ready")
        s_t2 = sem("xm_turned")
        s_xmT = sem("xmT_ready")
        s_l = sem("logits_done")
        s_lg = sem("logits_kept")
        s_out = [sem("rows_stored_0"), sem("rows_stored_1")]
        s_xs = [sem("xm_stored_0"), sem("xm_stored_1")]
        b_ls = sem("logits_in_scratch")
        b_ll = sem("logits_by_group")
        b_pm = sem("group_max_ready")
        b_sp = sem("spread_ready")
        b_sT = sem("spread_turned")
        b_ng = sem("ngmax_ready")
        b_no = sem("ngown_ready")
        b_ps = sem("prs_ready")
        b_ex = sem("prb_ready")
        b_su = sem("sum_done")
        b_pi = sem("pinv_ready")
        b_hl = sem("halves_ready")
        b_in = sem("search_set")
        b_ct = sem("counts_ready")
        b_tt = sem("totals_done")
        b_nx = sem("threshold_and_bits_ready")
        b_kb = sem("kept_bit_ready")
        b_ca = sem("candidate_ready")
        b_lw = sem("lower_halves_steps")
        b_th = sem("threshold_steps")
        b_gt = sem("above_ready")
        b_ga = sem("above_counted")
        b_eq = sem("equal_ready")
        b_nd = sem("need_ready")
        b_rk = sem("tie_ranks_done")
        b_sc = sem("scan_steps")
        b_se = sem("sel_ready")
        b_tb = sem("table_done")
        b_ta = sem("table_kept")
        b_pf = sem("first_ranks_done")
        b_fr = sem("first_ranks_kept")
        b_be = sem("begun_ready")
        b_lo = sem("lookup_done")
        b_sl = sem("slot_ready")
        b_pl = sem("place_ready")
        b_ro = sem("rows_ready")
        c_g = [sem("gathered_0"), sem("gathered_1"), sem("gathered_2")]
        c_t = sem("gathered_turned")
        c_gT = sem("gT_ready")
        c_v = sem("val_logits_done")
        c_ve = sem("val_exp_done")
        c_va = sem("val_ready")
        c_up = sem("expert_up_done")
        c_ge = sem("gelu_done")
        c_dn = sem("expert_down_done")
        c_yb = sem("y_biased")
        c_y = sem("y_ready")
        c_sc = [sem("rows_added_0"), sem("rows_added_1")]

        NW = 17

        def slot16(t, par):
            return 8 * (t - par) + 16

        def wait(eng, s, value):
            if not isinstance(value, int) or value > 0:
                eng.wait_ge(s, value)

        def steps(eng, step):
            for t in range(-2, 2):
                step(t, t % 2)
            with eng.Fori(2, PAIRS - 3, 2) as i:
                step(i, 0)
                step(i + 1, 1)
            for t in range(PAIRS - 2, PAIRS + 1):
                step(t, t % 2)

        def there(t):
            return not isinstance(t, int) or 0 <= t < PAIRS

        block = ctx.enter_context(nc.Block())

        @block.sync
        def _(sp):
            for dst, src in ((tokw_s, tok_w), (tokb_s, tok_b), (cls_s, cls), (pos_s, pos),
                             (ident_s, ident), (wup_s, w_up), (bup_s, b_up), (we2_s, w_e2),
                             (be2_s, b_e2), (wkq_s, w_kq), (bkq_s, b_kq), (wr_s, wr),
                             (upto_s, upto), (after_s, after), (before_s, before), (group_s, group),
                             (number_s, number)):
                sp.dma_start(dst[:], src).then_inc(s_w, 16)

            def load_x(t, par):
                wait(sp, s_proj, t - 1)
                sp.dma_start(xs[:, par], x[t]).then_inc(s_x[par], 16)

            def load_txt(t, par):
                wait(sp, s_h1, t - 1)
                sp.dma_start(h0[IMG_ROWS1:HALF, par, :, 1, :], txt[t]).then_inc(s_txt[par], 16)

            def store(t, par):
                wait(sp, s_h1, t + 1)
                sp.dma_start(pair_rows[t], h1[:, par]).then_inc(s_out[par], 16)

            for t in range(2):
                load_x(t, t)
                load_txt(t, t)
            for dst, src in ((rank_u, rank), (w1_s, w1), (b1_s, b1), (w2_s, w2), (b2_s, b2)):
                sp.dma_start(dst[:], src).then_inc(s_w2, 16)
            def store_xm(t, par):
                wait(sp, s_xm, t + 1)
                sp.dma_start(xm_pairs[t], xm[:, par]).then_inc(s_xs[par], 16)

            def step(t, par):
                if there(t + 3):
                    load_x(t + 3, 1 - par)
                if there(t - 1):
                    store_xm(t - 1, 1 - par)
                store(t, par)
                if there(t + 2):
                    load_txt(t + 2, par)

            load_x(2, 0)
            for t in range(2):
                step(t, t)
            with sp.Fori(2, PAIRS - 5, 2) as i:
                step(i, 0)
                step(i + 1, 1)
            for t in range(PAIRS - 4, PAIRS):
                step(t, t % 2)
            store_xm(PAIRS - 1, 1)
            sp.wait_ge(s_lg, PAIRS)
            sp.dma_start(lg_dram.rearrange("e (p c) -> p e c", c=COLS), lg[:]).then_inc(b_ls, 16)
            sp.wait_ge(b_ls, 16)
            sp.dma_start(lgs[:], lg_dram.rearrange("e (k n) -> (e k) n", n=GN)).then_inc(b_ll, 16)

        @block.tensor
        def _(pe):
            pe.wait_ge(s_w, 16 * NW)
            pe.wait_ge(s_ht0, 1)

            def project(t, par):
                pe.wait_ge(s_x[par], slot16(t, par))
                wait(pe, s_hT, t - 1)
                wait(pe, s_lg, t - 2)
                for k in range(PK):
                    last = pe.matmul(B[par][:, 0:2 * PATCHES], tokw_s[:, k, :], xs[:, par, k, :],
                                     start=(k == 0), stop=(k == PK - 1))
                last.then_inc(s_proj, 1)

            def turn_h(t, par):
                pe.wait_ge(s_hT, t + 1)
                wait(pe, s_k, t)
                wait(pe, s_q, t)
                for m in range(2):
                    pe.transpose(B[6][0:HALF, (2 * m) * D:(2 * m + 1) * D], hT[:, par, m, 0:HALF],
                                 ident_s[:])
                    last = pe.transpose(B[6][0:IMG_ROWS1, (2 * m + 1) * D:(2 * m + 2) * D],
                                        hT[:, par, m, HALF:HALF + IMG_ROWS1], ident_s[:])
                last.then_inc(s_t0, 1)

            def turn_rows(bank, src, done):
                for c in range(4):
                    last = pe.transpose(bank[:, c * HALF:(c + 1) * HALF], src[:, c, :],
                                        ident_s[0:HALF, 0:HALF])
                last.then_inc(done, 1)

            def up(t):
                pe.wait_ge(s_xnT, t + 1)
                for m in range(4):
                    if m == 0:
                        wait(pe, s_pa, t)
                    if m == 1:
                        wait(pe, s_pd, t)
                    if m == 2:
                        pe.wait_ge(s_ra, 3 * t + 1)
                    if m == 3:
                        pe.wait_ge(s_ra, 3 * t + 2)
                    pe.matmul(B[2 + m % 2][:, 0:2 * TOK], wup_s[:, m, :], xnT[:], start=True,
                              stop=True).then_inc(s_up, 1)

            def keys(t):
                pe.wait_ge(s_ra, 3 * t + 2)
                for m in range(2):
                    last = pe.matmul(B[6][:, 0:2 * TOK], wkq_s[:, m, :], hid[:, m, :],
                                     start=(m == 0), stop=(m == 1))
                last.then_inc(s_kq, 1)

            def embed(t):
                pe.wait_ge(s_ra, 3 * t + 3)
                pe.wait_ge(s_rd, t + 1)
                wait(pe, s_h1, t)
                for c in range(4):
                    for m in range(2):
                        last = pe.matmul(B[7][0:HALF, c * D:(c + 1) * D],
                                         hid[:, 2 + m, c * HALF:(c + 1) * HALF], we2_s[:, m, :],
                                         start=(m == 0), stop=(m == 1))
                last.then_inc(s_em, 1)

            def scores(t, m):
                if m == 0:
                    pe.wait_ge(s_k, t + 1)
                    pe.wait_ge(s_q, t + 1)
                    wait(pe, s_exp, 2 * t - 1)
                if m == 1:
                    wait(pe, s_xmT, t)
                for c in range(2):
                    at = m * TOK + c * HALF
                    last = pe.matmul(B[4 + m][0:HALF, c * TOK:(c + 1) * TOK],
                                     qT[:, at:at + HALF], kT[:, m * TOK:(m + 1) * TOK],
                                     start=True, stop=True)
                last.then_inc(s_sc, 1)

            def turn_xm(t, par):
                pe.wait_ge(s_xm, t + 1)
                turn_rows(B[5], xm[:, par], s_t2)

            def logits(t, par):
                pe.wait_ge(s_xmT, t + 1)
                wait(pe, s_hT, t + 2 if not isinstance(t, int) else min(t + 2, PAIRS))
                wait(pe, s_lg, t - 1)
                for c in range(4):
                    last = pe.matmul(B[1 - par][0:HALF, 384 + c * E:384 + (c + 1) * E],
                                     xmT[:, c * HALF:(c + 1) * HALF], wr_s[:], start=True, stop=True)
                last.then_inc(s_l, 1)

            def turn_prob(t):
                for m in range(2):
                    pe.wait_ge(s_exp, 2 * t + 1 + m)
                    for kh in range(2):
                        for qh in range(2):
                            last = pe.transpose(
                                B[2 + m][0:HALF, kh * TOK + qh * HALF:kh * TOK + (qh + 1) * HALF],
                                prob[:, 2 * m + qh, kh * HALF:(kh + 1) * HALF],
                                ident_s[0:HALF, 0:HALF])
                    last.then_inc(s_ta, 1)

            def attend(t):
                pe.wait_ge(s_emb, t + 1)
                for m in range(2):
                    pe.wait_ge(s_pa if m == 0 else s_pd, t + 1)
                    for qh in range(2):
                        c = 2 * m + qh
                        for kh in range(2):
                            last = pe.matmul(B[7 - 2 * m][0:HALF, qh * D:(qh + 1) * D],
                                             probT[:, m, kh, qh * HALF:(qh + 1) * HALF],
                                             emb[:, 2 * m + kh, :], start=(kh == 0), stop=(kh == 1))
                    last.then_inc(s_o, 1)

            def step(t, par):
                if there(t):
                    up(t)
                    keys(t)
                    embed(t)
                if there(t + 1):
                    turn_h(t + 1, 1 - par)
                if there(t - 1):
                    turn_xm(t - 1, 1 - par)
                if there(t):
                    scores(t, 0)
                if there(t - 1):
                    logits(t - 1, 1 - par)
                if there(t):
                    scores(t, 1)
                if there(t + 2):
                    project(t + 2, par)
                if there(t):
                    turn_prob(t)
                if there(t + 1):
                    pe.wait_ge(s_xn, t + 2)
                    turn_rows(B[6], xn, s_t1)
                if there(t):
                    attend(t)

            steps(pe, step)

            pe.wait_ge(s_const, 2)

            def turn_spread(n):
                pe.wait_ge(b_sp, n)
                pe.transpose(B[n % 2][:, 0:128], spread[:], ident_s[:]).then_inc(b_sT, 1)

            turn_spread(1)
            turn_spread(2)
            pe.wait_ge(b_ex, 1)
            pe.matmul(B[2][:, 0:E], ones_s[0:HALF, :], sum_p[:], start=True, stop=True).then_inc(b_su, 1)
            with pe.Fori(1, HI_BITS + LO_BITS + 1) as i:
                pe.wait_ge(b_ct, i)
                pe.matmul(B[3][:, 0:1], group_s[:], cnt[:], start=True, stop=True).then_inc(b_tt, 1)
            turn_spread(3)
            pe.wait_ge(b_gt, 1)
            pe.matmul(B[2][0:HALF, 0:E], ones_s[0:HALF, 0:HALF], cntg[:], start=True,
                      stop=True).then_inc(b_ga, 1)
            pe.wait_ge(b_eq, 1)
            pe.wait_ge(b_nd, 1)
            for e in range(E):
                pe.matmul(B[e][0:HALF, 0:COLS], after_b[:], eq[:, e, :], start=True, stop=True)
                pe.matmul(B[e][0:HALF, COLS:2 * COLS], ones_b[:], eq[:, e, :], start=True,
                          stop=True).then_inc(b_rk, 1)
            pe.wait_ge(b_se, 1)
            for w in range(2):
                for e in range(E):
                    for b in range(BLK):
                        at = 16 * w + b * E + e
                        last = pe.matmul(B[4][:, at:at + 1], sel[:, e, 1 - w + b * 128:1 - w + (b + 1) * 128],
                                         ones_b[:, 0:1], start=True, stop=True)
            last.then_inc(b_tb, 1)
            pe.wait_ge(b_se, 2)
            for e in range(E):
                for b in range(BLK):
                    at = (e % 2 * BLK + b) * HALF
                    last = pe.matmul(B[e // 2][:, at:at + HALF], dsel[:, e, b * 128:(b + 1) * 128],
                                     upto_b[:], start=True, stop=True)
            last.then_inc(b_tb, 1)
            pe.wait_ge(b_ta, 1)
            pe.matmul(B[5][:, 0:E], before_s[:], tot[:, 0, :], start=True, stop=True)
            pe.matmul(B[5][:, E:2 * E], before_s[:], tot[:, 1, :], start=True, stop=False)
            pe.matmul(B[5][:, E:2 * E], ones_s[:], tot[:, 0, :], start=False, stop=True).then_inc(b_pf, 1)
            pe.wait_ge(b_ta, 2)
            for e in range(E):
                pe.wait_ge(b_be, e + 1)
                if e >= 2:
                    pe.wait_ge(b_ro, e - 1)
                for c in range(CH):
                    for b in range(BLK):
                        last = pe.matmul(B[2 * (e % 2) + c // 4][:, (c % 4) * 96:(c % 4) * 96 + TW],
                                         begun[:, e % 2, b, c * 128:(c + 1) * 128], table[:, e, b, :],
                                         start=(b == 0), stop=(b == BLK - 1))
                last.then_inc(b_lo, 1)

            def turn_gathered(e):
                pe.wait_ge(c_g[e % 3], 16 * CH * (e // 3 + 1))
                if e == 0:
                    pe.wait_ge(b_ro, E)
                else:
                    pe.wait_ge(c_gT, 2 * e)
                    pe.wait_ge(c_ve, e)
                for q in range(2):
                    for c in range(4):
                        last = pe.transpose(B[q][:, c * 128:(c + 1) * 128], g[:, e % 3, 4 * q + c, :],
                                            ident_s[:])
                    last.then_inc(c_t, 1)

            def val_logits(e):
                pe.wait_ge(c_gT, 2 * e + 2)
                for c in range(CH):
                    last = pe.matmul(B[0][:, c:c + 1], gT[:, e % 2, c, :], wr_s[:, e:e + 1],
                                     start=True, stop=True)
                last.then_inc(c_v, 1)

            def expert_up(n):
                e, q = n // 2, n % 2
                for f in range(FT):
                    k = n * FT + f
                    if k >= 4:
                        pe.wait_ge(c_ge, k - 3)
                    pe.matmul(B[2 + k % 4][:, :], w1_s[:, e, f * 128:(f + 1) * 128],
                              gT[:, e % 2, 4 * q:4 * q + 4, :], start=True, stop=True).then_inc(c_up, 1)

            def expert_down(n):
                e = n // 2
                pe.wait_ge(c_ge, FT * (n + 1))
                if n >= 2:
                    pe.wait_ge(c_yb, n - 1)
                for c in range(4):
                    for f in range(FT):
                        last = pe.matmul(B[6 + n % 2][:, c * D:(c + 1) * D],
                                         act1[:, n % 2, f, c * 128:(c + 1) * 128], w2_s[:, e, f, :],
                                         start=(f == 0), stop=(f == FT - 1))
                last.then_inc(c_dn, 1)

            pe.wait_ge(s_w2, 16 * 5)
            turn_gathered(0)
            val_logits(0)
            for n in range(2 * E):
                ahead = n // 2 + 1 if n % 2 == 0 and n // 2 + 1 < E else None
                expert_up(n)
                if ahead is not None:
                    turn_gathered(ahead)
                if n >= 1:
                    expert_down(n - 1)
                if ahead is not None:
                    val_logits(ahead)
            expert_down(2 * E - 1)

        @block.scalar
        def _(act):
            act.wait_ge(s_w, 16 * NW)
            for par in range(2):
                for m in range(2):
                    last = act.copy(hT[:, par, m, 0:1], cls_s[:])
            last.then_inc(s_ht0, 1)

            def keep_hT(t, par):
                act.wait_ge(s_proj, t + 1)
                wait(act, s_t0, t - 1)
                act.activation(hT[:, par, :, 1:1 + PATCHES],
                               B[par][:, 0:2 * PATCHES].rearrange("p (m n) -> p m n", m=2),
                               ACT.Identity, bias=tokb_s[:]).then_inc(s_hT, 1)

            def relus(t):
                for m in range(3):
                    act.wait_ge(s_up, 4 * t + 1 + m)
                    wait(act, s_kq if m < 2 else s_em, t)
                    act.activation(hid[:, m, :], B[2 + m % 2][:, 0:2 * TOK], ACT.Relu,
                                   bias=bup_s[:, m:m + 1]).then_inc(s_ra, 1)

            def keep_k(t):
                act.wait_ge(s_kq, t + 1)
                wait(act, s_sc, 2 * t)
                act.activation(kT[:], B[6][0:DA, 0:2 * TOK], ACT.Identity,
                               bias=bkq_s[0:DA, :]).then_inc(s_k, 1)

            def keep_xmT(t):
                act.wait_ge(s_t2, t + 1)
                wait(act, s_l, t)
                act.copy(xmT[:], B[5][:, 0:2 * TOK]).then_inc(s_xmT, 1)

            def keep_logits(t, par):
                act.wait_ge(s_l, t + 1)
                act.copy(lg[:, :, bass.ds(4 * t, 4)].rearrange("p e c -> p c e"),
                         B[1 - par][0:HALF, 384:384 + 4 * E].rearrange("p (c e) -> p c e", c=4)
                         ).then_inc(s_lg, 1)

            def exps(t):
                for m in range(2):
                    act.wait_ge(s_nm, 2 * t + 1 + m)
                    if m == 0:
                        wait(act, s_ta, 2 * t)
                        wait(act, s_ri, t)
                    for c in range(2):
                        k = 2 * m + c
                        last = act.activation(prob[:, k, :], B[4 + m][0:HALF, c * TOK:(c + 1) * TOK],
                                              ACT.Exp, bias=nmax[:, k:k + 1],
                                              accum_out=rsum[:, k:k + 1])
                    last.then_inc(s_exp, 1)

            def keep_probT(t):
                act.wait_ge(s_ta, 2 * t + 1)
                wait(act, s_o, 2 * t)
                act.copy(probT[:, 0, :, :], B[2][0:HALF, 0:2 * TOK].rearrange("p (k q) -> p k q", k=2)
                         ).then_inc(s_pa, 1)

            def keep_xnT(t):
                act.wait_ge(s_t1, t + 1)
                wait(act, s_up, 4 * t)
                act.copy(xnT[:], B[6][:, 0:2 * TOK]).then_inc(s_xnT, 1)

            def step(t, par):
                if there(t):
                    relus(t)
                    keep_k(t)
                if there(t - 1):
                    keep_xmT(t - 1)
                    keep_logits(t - 1, 1 - par)
                if there(t):
                    exps(t)
                if there(t + 2):
                    keep_hT(t + 2, par)
                if there(t):
                    keep_probT(t)
                if there(t + 1):
                    keep_xnT(t + 1)

            steps(act, step)

            act.wait_ge(b_no, 1)
            act.activation(prs[:], lgs[:], ACT.Exp, bias=ngown[:]).then_inc(b_ps, 1)
            for e in range(E):
                last = act.activation(prb[:, e, :], lg[:, e, :], ACT.Exp, bias=ngmax[0:HALF, e:e + 1],
                                      accum_out=sum_p[:, e:e + 1])
            last.then_inc(b_ex, 1)

            def keep_gT(e):
                if e >= 2:
                    act.wait_ge(c_up, 2 * FT * (e - 1))
                    act.wait_ge(c_v, e - 1)
                for q in range(2):
                    act.wait_ge(c_t, 2 * e + q + 1)
                    act.copy(gT[:, e % 2, 4 * q:4 * q + 4, :], B[q][:].rearrange("p (c n) -> p c n", c=4)
                             ).then_inc(c_gT, 1)
                act.wait_ge(c_v, e + 1)
                act.activation(vexp[:, e, :], B[0][:, 0:CH], ACT.Exp, bias=ngmax[:, e:e + 1]
                               ).then_inc(c_ve, 1)

            act.wait_ge(s_w2, 16 * 5)
            keep_gT(0)
            for n in range(2 * E):
                if n >= 2:
                    act.wait_ge(c_dn, n - 1)
                for f in range(FT):
                    k = n * FT + f
                    act.wait_ge(c_up, k + 1)
                    act.activation(act1[:, n % 2, f, :], B[2 + k % 4][:, :], ACT.Gelu,
                                   bias=b1_s[:, n // 2, f:f + 1]).then_inc(c_ge, 1)
                if n % 2 == 0 and n // 2 + 1 < E:
                    keep_gT(n // 2 + 1)

        @block.vector
        def _(dve):
            dve.memset(ones_s[:], 1.0)
            dve.memset(ones_b[:], 1.0)
            dve.memset(half_s[:], -0.5)
            dve.memset(eps_s[:], EPS)
            dve.memset(zero_s[:], 0.0).then_inc(s_const, 1)
            dve.wait_ge(s_w, 16 * NW)
            dve.tensor_copy(upto_b[:], upto_s[:])
            dve.tensor_copy(after_b[:], after_s[:]).then_inc(s_const, 1)

            def relu(t):
                dve.wait_ge(s_up, 4 * t + 4)
                wait(dve, s_em, t)
                dve.tensor_scalar(hid[:, 3, :], B[3][:, 0:2 * TOK], bup_s[:, 3:4], 0.0,
                                  ALU.add, ALU.max).then_inc(s_rd, 1)

            def keep_q(t):
                dve.wait_ge(s_kq, t + 1)
                wait(dve, s_sc, 2 * t)
                dve.tensor_scalar(qT[:], B[6][DA:2 * DA, 0:2 * TOK], bkq_s[DA:2 * DA, :], None,
                                  ALU.add).then_inc(s_q, 1)

            def keep_emb(t):
                dve.wait_ge(s_em, t + 1)
                dve.tensor_tensor(emb[:], B[7][0:HALF, :].rearrange("p (c d) -> p c d", c=4),
                                  be2_s[0:HALF, :].unsqueeze(1).to_broadcast([HALF, 4, D]),
                                  ALU.add).then_inc(s_emb, 1)

            def maxima(t, m):
                dve.wait_ge(s_sc, 2 * t + 1 + m)
                wait(dve, s_exp, 2 * t)
                dve.tensor_reduce(nmax[:, 2 * m:2 * m + 2],
                                  B[4 + m][0:HALF, 0:2 * TOK].rearrange("p (c k) -> p c k", c=2),
                                  AX.X, ALU.max, negate=True).then_inc(s_nm, 1)

            def stats(t, rows, st, mv, ready, s_st, s_mv, used):
                wait(dve, used, t)
                for c in range(4):
                    last = dve.bn_stats(st[:, c, :], rows[:, c, :])
                last.then_inc(s_st, 1)
                dve.wait_ge(s_const, 1)
                dve.wait_ge(s_st, t + 1)
                for c in range(4):
                    last = dve.bn_aggr(mv[:, c, :], st[:, c, :])
                last.then_inc(s_mv, 1)

            def normalise(t, n, rows, mv, rs, outs, s_r, done):
                dve.wait_ge(s_const, 1)
                dve.wait_ge(s_r, t + 1)
                for c in range(n):
                    last = dve.tensor_scalar(outs[:, c, :], rows[:, c, :], mv[:, c, 0:1],
                                             rs[:, 1, c:c + 1], ALU.subtract, ALU.mult)
                last.then_inc(done, 1)

            def normalise_h0(t, par):
                wait(dve, s_t1, t)
                normalise(t, 4, h0[:, par].rearrange("p m c d -> p (m c) d"), mv1, rs1, xn, s_r1[1], s_xn)

            def normalise_h1(t, par):
                wait(dve, s_t2, t - 1)
                wait(dve, s_xs[par], slot16(t - 2, par))
                normalise(t, 4, h1[:, par], mv2, rs2, xm[:, par], s_r2[1], s_xm)

            def keep_h0(t, par):
                dve.wait_ge(s_t0, t + 1)
                turned = B[6][:, :].rearrange("p (m c d) -> p m c d", m=2, c=2)
                dve.tensor_scalar(h0[:, par, :, 0, :], turned[0:HALF, :, 0, :], pos_s[:, 0:1], None,
                                  ALU.add)
                dve.tensor_scalar(h0[0:IMG_ROWS1, par, :, 1, :], turned[0:IMG_ROWS1, :, 1, :],
                                  pos_s[0:IMG_ROWS1, 1:2], None, ALU.add).then_inc(s_h0, 1)
                dve.wait_ge(s_h0, t + 1)
                dve.wait_ge(s_txt[par], slot16(t, par))
                stats(t, h0[:, par].rearrange("p m c d -> p (m c) d"), st1, mv1, s_h0, s_st1, s_mv1,
                      s_xn)

            def keep_probT(t):
                dve.wait_ge(s_ta, 2 * t + 2)
                wait(dve, s_o, 2 * t)
                dve.tensor_copy(probT[:, 1, :, :],
                                B[3][0:HALF, 0:2 * TOK].rearrange("p (k q) -> p k q", k=2)
                                ).then_inc(s_pd, 1)
                dve.reciprocal(rinv[:], rsum[:]).then_inc(s_ri, 1)

            def residual(t, par):
                dve.wait_ge(s_ri, t + 1)
                wait(dve, s_out[par], slot16(t - 2, par))
                wait(dve, s_xm, t - 1)
                for c in range(4):
                    if c % 2 == 0:
                        dve.wait_ge(s_o, 2 * t + 1 + c // 2)
                    last = dve.scalar_tensor_tensor(out=h1[:, par, c, :], 
                                                    in0=B[7 - c // 2 * 2][0:HALF, c % 2 * D:(c % 2 + 1) * D],
                                                    scalar=rinv[:, c:c + 1], in1=h0[:, par, c // 2, c % 2, :],
                                                    op0=ALU.mult, op1=ALU.add)
                last.then_inc(s_h1, 1)
                dve.wait_ge(s_h1, t + 1)
                stats(t, h1[:, par], st2, mv2, s_h1, s_st2, s_mv2, s_xm)

            def step(t, par):
                if there(t):
                    relu(t)
                if there(t - 1):
                    normalise_h1(t - 1, 1 - par)
                if there(t):
                    keep_q(t)
                    keep_emb(t)
                if there(t + 1):
                    keep_h0(t + 1, 1 - par)
                if there(t):
                    maxima(t, 0)
                if there(t):
                    maxima(t, 1)
                if there(t + 1):
                    normalise_h0(t + 1, 1 - par)
                if there(t):
                    keep_probT(t)
                    residual(t, par)

            steps(dve, step)

            dve.wait_ge(s_w2, 16 * 5)
            dve.memset(sel[:, :, 0:1], 0.0).then_inc(s_const, 1)
            dve.wait_ge(s_const, 3)
            dve.wait_ge(b_ll, 16)
            dve.tensor_reduce(pmax[:], lgs[:], AX.X, ALU.max).then_inc(b_pm, 1)
            dve.wait_ge(b_pm, 1)
            dve.tensor_copy(spread[:], pmax[:].to_broadcast([128, 128])).then_inc(b_sp, 1)
            dve.wait_ge(b_sT, 1)
            dve.tensor_reduce(ngmax[:], B[1][:, 0:128].rearrange("p (e k) -> p e k", e=E), AX.X, ALU.max,
                              negate=True).then_inc(b_ng, 1)
            dve.wait_ge(b_ng, 1)
            dve.tensor_copy(spread[:].rearrange("p (e k) -> p e k", e=E),
                            ngmax[:].unsqueeze(2).to_broadcast([128, E, GRP])).then_inc(b_sp, 1)
            dve.wait_ge(b_sT, 2)
            dve.tensor_copy(ngown[:], B[0][:, 0:1]).then_inc(b_no, 1)

            def start_search(bits):
                dve.memset(kbit[:], 0.0)
                dve.memset(bit[:], float(1 << bits))
                dve.memset(nbit[:], float(1 << (bits - 1)))
                dve.memset(cand[:], float(1 << (bits - 1))).then_inc(b_in, 1)

            def search(numbers, t, first, last):
                with dve.Fori(first, last + 1) as i:
                    dve.tensor_scalar(reach[:], numbers, cand[:], None, ALU.is_ge, ALU.add,
                                      accum_out=cnt[:]).then_inc(b_ct, 1)
                    dve.tensor_tensor(t, t, kbit[:], ALU.add)
                    dve.tensor_scalar(bit[:], bit[:], 0.5, None, ALU.mult)
                    dve.tensor_scalar(nbit[:], nbit[:], 0.5, None, ALU.mult).then_inc(b_nx, 1)
                    dve.wait_ge(b_nx, i)
                    dve.wait_ge(b_tt, i)
                    dve.tensor_scalar(kbit[:], B[3][:, 0:1], float(CAP), bit[:], ALU.is_ge,
                                      ALU.mult).then_inc(b_kb, 1)
                    dve.wait_ge(b_kb, i)
                    dve.scalar_tensor_tensor(out=cand[:], in0=kbit[:], scalar=nbit[:], in1=t, op0=ALU.add,
                                             op1=ALU.add).then_inc(b_ca, 1)
                    dve.wait_ge(b_ca, i)

            dve.memset(thr[:], 0.0)
            start_search(HI_BITS)
            dve.wait_ge(b_in, 1)
            dve.wait_ge(b_ps, 1)
            halves = prs[:].bitcast(u16).rearrange("p (n h) -> p h n", h=2)
            dve.tensor_copy(hi[:], halves[:, 1, :]).then_inc(b_hl, 1)
            dve.wait_ge(b_hl, 1)
            search(hi[:], thr[:, 0:1], 1, HI_BITS)
            dve.tensor_tensor(thr[:, 0:1], thr[:, 0:1], kbit[:], ALU.add).then_inc(b_th, 1)
            dve.wait_ge(b_th, 1)
            start_search(LO_BITS)
            dve.tensor_scalar(above[:], hi[:], thr[:, 0:1], 65535.0, ALU.is_gt, ALU.mult)
            dve.scalar_tensor_tensor(out=lo[:], in0=hi[:], scalar=thr[:, 0:1], in1=halves[:, 0, :],
                                     op0=ALU.is_equal, op1=ALU.mult).then_inc(b_lw, 1)
            dve.wait_ge(b_lw, 1)
            dve.wait_ge(b_in, 2)
            dve.tensor_tensor(lo[:], lo[:], above[:], ALU.max).then_inc(b_lw, 1)
            dve.wait_ge(b_lw, 2)
            search(lo[:], thr[:, 1:2], HI_BITS + 1, HI_BITS + LO_BITS)
            dve.tensor_tensor(thr[:, 1:2], thr[:, 1:2], kbit[:], ALU.add).then_inc(b_th, 1)
            dve.wait_ge(b_th, 2)
            dve.tensor_copy(thr_i[:], thr[:]).then_inc(b_th, 1)
            dve.wait_ge(b_th, 3)
            dve.scalar_tensor_tensor(out=thr_b[:], in0=thr_i[:, 0:1], scalar=16, in1=thr_i[:, 1:2],
                                     op0=ALU.logical_shift_left, op1=ALU.bitwise_or).then_inc(b_th, 1)
            dve.wait_ge(b_th, 4)
            dve.tensor_copy(spread[:].bitcast(i32), thr_b[:].to_broadcast([128, 128])).then_inc(b_sp, 1)
            dve.wait_ge(b_su, 1)
            dve.reciprocal(pinv[:], B[2][:, 0:E]).then_inc(b_pi, 1)
            dve.wait_ge(b_sT, 3)
            dve.tensor_copy(limit[:].bitcast(i32), B[1][0:HALF, 0:128:GRP].bitcast(i32)).then_inc(b_th, 1)
            dve.wait_ge(b_th, 5)
            dve.wait_ge(b_pi, 1)

            for e in range(E):
                last = dve.tensor_scalar(gt[:, e, :], prb[:, e, :], limit[:, e:e + 1], None, ALU.is_gt,
                                         ALU.add, accum_out=cntg[:, e:e + 1])
            last.then_inc(b_gt, 1)
            for e in range(E):
                last = dve.tensor_scalar(eq[:, e, :], prb[:, e, :], limit[:, e:e + 1], None, ALU.is_equal)
            last.then_inc(b_eq, 1)
            dve.wait_ge(b_ga, 1)
            dve.tensor_scalar(need[:], B[2][0:HALF, 0:E], -1.0, float(CAP), ALU.mult, ALU.add).then_inc(b_nd, 1)
            for e in range(E):
                dve.wait_ge(b_rk, e + 1)
                last = dve.tensor_tensor_scan(scan[:, e, :], zero_s[:], B[e][0:HALF, COLS:2 * COLS], 0.0,
                                              ALU.add, ALU.add)
            last.then_inc(b_sc, 1)
            dve.wait_ge(b_sc, 1)
            for e in range(E):
                last = dve.tensor_tensor(rk[:, e, :], scan[:, e, :], B[e][0:HALF, 0:COLS], ALU.add)
            last.then_inc(b_sc, 1)
            dve.wait_ge(b_sc, 2)
            dve.wait_ge(b_nd, 1)
            dve.wait_ge(b_eq, 1)
            for e in range(E):
                last = dve.scalar_tensor_tensor(out=tie[:, e, :], in0=rk[:, e, :], scalar=need[:, e:e + 1],
                                                in1=eq[:, e, :], op0=ALU.is_le, op1=ALU.mult)
            last.then_inc(b_sc, 1)
            dve.wait_ge(b_sc, 3)
            dve.wait_ge(b_gt, 1)
            dve.tensor_tensor(sel[:, :, 1:], tie[:], gt[:], ALU.add).then_inc(b_se, 1)
            dve.wait_ge(b_se, 1)
            dve.tensor_tensor(dsel[:], sel[:, :, 1:], sel[:, :, 0:COLS], ALU.subtract).then_inc(b_se, 1)
            dve.wait_ge(b_tb, 1)
            dve.tensor_copy(tot[:], B[4][:, 0:2 * E].rearrange("p (b e) -> p b e", b=BLK)).then_inc(b_ta, 1)
            dve.tensor_copy(table[:, :, :, HALF], B[4][:, 2 * E:4 * E].rearrange("p (b e) -> p e b", b=BLK))
            dve.tensor_copy(table[:, :, :, HALF + 1],
                            number_s[:, CH:CH + BLK].unsqueeze(1).to_broadcast([128, E, BLK]))
            dve.wait_ge(b_tb, 2)
            for k in range(E // 2):
                last = dve.tensor_copy(table[:, 2 * k:2 * k + 2, :, 0:HALF],
                                       B[k][:, 0:4 * HALF].rearrange("p (e b n) -> p e b n", e=2, b=BLK))
            last.then_inc(b_ta, 1)
            dve.wait_ge(b_pf, 1)
            dve.tensor_copy(first[:], B[5][:, 0:2 * E].rearrange("p (b e) -> p b e", b=BLK)).then_inc(b_fr, 1)
            dve.wait_ge(b_fr, 1)

            def columns_begun(e):
                if e >= 2:
                    dve.wait_ge(b_lo, e - 1)
                for b in range(BLK):
                    last = dve.tensor_scalar(begun[:, e % 2, b, :], rank_u[:], first[:, b, e:e + 1], None,
                                             ALU.is_ge)
                last.then_inc(b_be, 1)

            def find_rows(e):
                k = e % 2
                dve.wait_ge(b_lo, e + 1)
                for q in range(2):
                    looked = B[2 * k + q][:, 0:384].rearrange("p (c n) -> p c n", c=4)
                    last = dve.tensor_tensor(slot[:, k, 4 * q:4 * q + 4], number_s[:, 4 * q:4 * q + 4],
                                             looked[:, :, HALF], ALU.subtract)
                last.then_inc(b_sl, 1)
                dve.wait_ge(b_sl, e + 1)
                for c in range(CH):
                    at = (c % 4) * 96
                    last = dve.tensor_scalar(passed[:, c, :], B[2 * k + c // 4][:, at:at + HALF],
                                             slot[:, k, c:c + 1], None, ALU.is_le, ALU.add,
                                             accum_out=place[:, k, c:c + 1])
                last.then_inc(b_pl, 1)
                dve.wait_ge(b_pl, e + 1)
                for q in range(2):
                    looked = B[2 * k + q][:, 0:384].rearrange("p (c n) -> p c n", c=4)
                    last = dve.scalar_tensor_tensor(out=row[:, e, 4 * q:4 * q + 4],
                                                    in0=looked[:, :, HALF + 1], scalar=float(HALF),
                                                    in1=place[:, k, 4 * q:4 * q + 4], op0=ALU.mult, op1=ALU.add)
                last.then_inc(b_ro, 1)

            columns_begun(0)
            for e in range(E):
                if e + 1 < E:
                    columns_begun(e + 1)
                find_rows(e)

            def values(e):
                dve.wait_ge(c_ve, e + 1)
                dve.tensor_scalar(val[:, e, :], vexp[:, e, :], pinv[:, e:e + 1], None, ALU.mult
                                  ).then_inc(c_va, 1)

            def weigh(n):
                e, q = n // 2, n % 2
                dve.wait_ge(c_dn, n + 1)
                if n >= 4:
                    dve.wait_ge(c_sc[e % 2], 16 * CH * (e // 2))
                dve.tensor_tensor(y[:, n % 4], B[6 + n % 2][:].rearrange("p (c d) -> p c d", c=4),
                                  b2_s[:, e, :].unsqueeze(1).to_broadcast([128, 4, D]),
                                  ALU.add).then_inc(c_yb, 1)
                dve.wait_ge(c_yb, n + 1)
                dve.wait_ge(c_va, e + 1)
                dve.tensor_tensor(y[:, n % 4], y[:, n % 4],
                                  val[:, e, 4 * q:4 * q + 4].unsqueeze(2).to_broadcast([128, 4, D]),
                                  ALU.mult).then_inc(c_y, 1)

            values(0)
            for n in range(2 * E):
                if n >= 1:
                    weigh(n - 1)
                if n % 2 == 0 and n // 2 + 1 < E:
                    values(n // 2 + 1)
            weigh(2 * E - 1)

        @block.gpsimd
        def _(pool):
            pool.wait_ge(s_const, 1)

            def rstd(t, n, mv, rs, s_r):
                pool.tensor_tensor(rs[:, 0, :], mv[:, :, 1], eps_s[0:rs.shape[0], 0:n], ALU.add).then_inc(s_r[0], 1)
                pool.wait_ge(s_r[0], t + 1)
                pool.tensor_tensor(rs[:, 1, :], rs[:, 0, :], half_s[0:rs.shape[0], 0:n], ALU.pow).then_inc(s_r[1], 1)

            def step(t, par):
                if there(t - 1):
                    pool.wait_ge(s_mv2, t)
                    wait(pool, s_xm, t - 1)
                    rstd(t - 1, 4, mv2, rs2, s_r2)
                if there(t + 1):
                    pool.wait_ge(s_mv1, t + 2)
                    wait(pool, s_xn, t + 1)
                    rstd(t + 1, 4, mv1, rs1, s_r1)

            steps(pool, step)

            for par in range(2):
                pool.wait_ge(s_xs[par], 16 * (PAIRS // 2))
                pool.wait_ge(s_out[par], 16 * (PAIRS // 2))

            def gather(e):
                pool.wait_ge(b_ro, e + 1)
                if e >= 3:
                    pool.wait_ge(c_t, 2 * e - 4)
                for c in range(CH):
                    pool.indirect_dma_start(out=g[:, e % 3, c, :], out_offset=None, in_=xm_dram,
                                            in_offset=bass.IndirectOffsetOnAxis(ap=row[:, e, c:c + 1], axis=0)
                                            ).then_inc(c_g[e % 3], 16)

            def add_rows(n):
                e, q = n // 2, n % 2
                pool.wait_ge(c_y, n + 1)
                if q == 0 and e >= 1:
                    pool.wait_ge(c_sc[(e - 1) % 2], 16 * CH * ((e - 1) // 2 + 1))
                for c in range(4):
                    pool.indirect_dma_start(out=rows_dram, in_=y[:, n % 4, c, :], in_offset=None,
                                            out_offset=bass.IndirectOffsetOnAxis(
                                                ap=row[:, e, 4 * q + c:4 * q + c + 1], axis=0),
                                            compute_op=ALU.add).then_inc(c_sc[e % 2], 16)

            gather(0)
            gather(1)
            for e in range(E):
                if e + 2 < E:
                    gather(e + 2)
                add_rows(2 * e)
                add_rows(2 * e + 1)
            for k in range(2):
                pool.wait_ge(c_sc[k], 16 * CH * (E // 2))


def kernel(x, txt, L0_tok_W, L0_tok_b, L0_tok_cls_token, L0_tok_pos_emb, L0_attn_We1, L0_attn_be1,
           L0_attn_We2, L0_attn_be2, L0_attn_Wk1, L0_attn_bk1, L0_attn_Wk2, L0_attn_bk2, L0_ffn_Wr,
           L0_ffn_W1, L0_ffn_b1, L0_ffn_W2, L0_ffn_b2):
    import numpy as np
    import concourse.bacc as bacc
    from concourse.bass_utils import run_bass_kernel_spmd

    def a(v):
        return np.asarray(v)

    def tiles(v, n):
        return v.reshape((n, 128) + v.shape[1:]).swapaxes(0, 1)

    p = a(x).reshape(PAIRS, 2, 3, 11, 16, 13, 16).transpose(0, 4, 6, 2, 1, 3, 5)
    p = p.reshape(PAIRS, PK, 128, 2 * PATCHES).transpose(0, 2, 1, 3)
    pos = a(L0_tok_pos_emb).reshape(1 + PATCHES)
    pos2 = np.zeros((HALF, 2), pos.dtype)
    pos2[:, 0] = pos[:HALF]
    pos2[:IMG_ROWS1, 1] = pos[HALF:]
    w_up = np.concatenate([a(L0_attn_Wk1), a(L0_attn_We1)], 1).reshape(D, 4, 128)
    b_up = np.concatenate([a(L0_attn_bk1), a(L0_attn_be1)]).reshape(4, 128).T
    n = np.arange(128)
    ins = {
        "x": p,
        "txt": a(txt).reshape(PAIRS, 2, TXT, D).transpose(0, 2, 1, 3),
        "tok_w": tiles(a(L0_tok_W).T, PK),
        "tok_b": a(L0_tok_b).reshape(D, 1),
        "cls": a(L0_tok_cls_token).reshape(D, 1),
        "pos": pos2,
        "w_up": w_up,
        "b_up": b_up,
        "w_e2": tiles(a(L0_attn_We2), 2),
        "b_e2": np.broadcast_to(a(L0_attn_be2), (128, D)),
        "w_kq": tiles(a(L0_attn_Wk2), 2),
        "b_kq": a(L0_attn_bk2).reshape(128, 1),
        "wr": a(L0_ffn_Wr),
        "w1": a(L0_ffn_W1).transpose(1, 0, 2),
        "b1": a(L0_ffn_b1).reshape(E, FT, 128).transpose(2, 0, 1),
        "w2": a(L0_ffn_W2).reshape(E, FT, 128, D).transpose(2, 0, 1, 3),
        "b2": np.broadcast_to(a(L0_ffn_b2), (128, E, D)),
        "ident": np.eye(128, dtype=np.float32),
        "upto": (n[:HALF, None] <= n[None, :HALF]).astype(np.float32),
        "after": -(n[:HALF, None] > n[None, :HALF]).astype(np.float32),
        "before": (n[:, None] < n[None, :]).astype(np.float32),
        "group": (n[:, None] // GRP == n[None, :] // GRP).astype(np.float32),
        "rank": np.broadcast_to(np.arange(CAP, dtype=np.uint16), (128, CAP)),
        "number": np.concatenate([n[:, None] + 128 * np.arange(CH)[None, :],
                                  n[:, None] + 128 * np.arange(BLK)[None, :] > 0], 1).astype(np.float32),
    }
    ins = {"in_" + k: np.ascontiguousarray(v) for k, v in ins.items()}
    nc = bacc.Bacc("TRN2", target_bir_lowering=False, num_devices=1)
    args = [nc.dram_tensor(k, v.shape, mybir.dt.from_np(v.dtype), kind="ExternalInput").ap()
            for k, v in ins.items()]
    out = nc.dram_tensor("out", (IMGS, TOK, D), mybir.dt.float32, kind="ExternalOutput").ap()
    fusion_program(nc, *args, out)
    r = run_bass_kernel_spmd(nc, [ins], core_ids=[0])
    return r.results[0]["out"]
```

```python
import concourse.bass as bass
from concourse import mybir
from contextlib import ExitStack
import numpy as np

IMGS = 128
PATCHES = 143
TXT = 32
TOK = 1 + PATCHES + TXT
HALF = TOK // 2
D = 128
PK = 6
PAIRS = IMGS // 2
IMG_ROWS1 = 1 + PATCHES - HALF
HID = 256
DA = 64
E = 8
F = 512
FT = F // 128
CAP = 1024
CH = CAP // 128
COLS = 2 * IMGS
BLK = COLS // 128
EPS = 1e-5
GRP = 128 // E
GN = HALF * COLS // GRP
LATE = 32
SPLIT = HALF * (COLS - LATE) // GRP
HI_BITS = 14
LO_BITS = 16
HI_STEPS = HI_BITS // 2
STEPS = (HI_BITS + LO_BITS) // 2
BIG = 1 << 16
RANKED = (0, 1, 3, 4, 5, 6, 7, 2)
LOOK = 4
RING = 3
TW = HALF + 2


def fusion_program(nc, x, txt, tok_w, tok_b, cls, pos, w_up, b_up, w_e2, b_e2, w_kq, b_kq,
                   wr, w1, b1, w2, b2, ident, upto, after, before, group, rank, number, out):
    f32, bf16, i32, u16 = mybir.dt.float32, mybir.dt.bfloat16, mybir.dt.int32, mybir.dt.uint16
    f32r = mybir.dt.float32r
    ALU = mybir.AluOpType
    ACT = mybir.ActivationFunctionType
    AX = mybir.AxisListType

    pair_rows = out.rearrange("(t m) (c p) d -> t p (m c) d", m=2, c=2)
    rows_dram = out.rearrange("i n d -> (i n) d")
    xm_dram = nc.dram_tensor("xm_dram", (IMGS * TOK, D), mybir.dt.float32, kind="Internal").ap()
    xm_pairs = xm_dram.rearrange("(t c p) d -> t p c d", c=4, p=HALF)
    lg_dram = [nc.dram_tensor(name, (E, HALF * n), mybir.dt.float32, kind="Internal").ap()
               for name, n in (("lg_early", COLS - LATE), ("lg_late", LATE))]

    ctx = ExitStack()
    with ctx:
        def sb(name, shape, dt=f32):
            return ctx.enter_context(nc.sbuf_tensor(name, shape, dt))

        def sem(name):
            return ctx.enter_context(nc.semaphore(name))

        ident_s = sb("ident_s", [128, 128])
        upto_s = sb("upto_s", [HALF, HALF])
        after_s = sb("after_s", [HALF, HALF])
        before_s = sb("before_s", [128, 128])
        group_s = sb("group_s", [128, 128])
        rank_u = sb("rank_u", [128, CAP], u16)
        number_s = sb("number_s", [128, CH + BLK])
        upto_b = sb("upto_b", [HALF, HALF], bf16)
        after_b = sb("after_b", [HALF, HALF], bf16)
        ones_b = sb("ones_b", [HALF, HALF], bf16)
        ones_s = sb("ones_s", [128, 128])
        eps_s = sb("eps_s", [128, 8])
        half_s = sb("half_s", [128, 8])
        tokw_s = sb("tokw_s", [128, PK, D])
        tokb_s = sb("tokb_s", [D, 1])
        cls_s = sb("cls_s", [D, 1])
        pos_s = sb("pos_s", [HALF, 2])
        wup_s = sb("wup_s", [D, 4, 128])
        bup_s = sb("bup_s", [128, 4])
        we2_s = sb("we2_s", [128, 2, D])
        be2_s = sb("be2_s", [128, D])
        wkq_s = sb("wkq_s", [128, 2, 128])
        bkq_s = sb("bkq_s", [128, 1])
        wr_s = sb("wr_s", [D, E])
        sizes = (PK * D, PK * D, PK * 2 * PATCHES, PK * 2 * PATCHES, 4 * TOK, 4 * TOK)
        parts = sb("parts", [128, sum(sizes)], f32r)
        ends = np.cumsum((0,) + sizes)
        part = [parts[:, a:b] for a, b in zip(ends[:-1].tolist(), ends[1:].tolist())]
        tokw_hi, tokw_lo = [p.rearrange("p (k d) -> p k d", k=PK) for p in part[0:2]]
        wup_hi = sb("wup_hi", [D, 4, 128], f32r)
        wup_lo = sb("wup_lo", [D, 4, 128], f32r)
        wkq_hi = sb("wkq_hi", [128, 2, 128], f32r)
        wkq_lo = sb("wkq_lo", [128, 2, 128], f32r)
        w1_s = sb("w1_s", [D, E, F])
        b1_s = sb("b1_s", [128, E, FT])
        w2_s = sb("w2_s", [128, E, FT, D])
        b2_s = sb("b2_s", [128, E, D])

        xs = sb("xs", [128, 2, PK, 2 * PATCHES])
        xs_hi, xs_lo = [p.rearrange("p (k n) -> p k n", k=PK) for p in part[2:4]]
        shared = sb("shared", [128, 2 * FT * 512])
        hid = shared[:, 0:8 * TOK].rearrange("p (m n) -> p m n", m=4)
        hT = shared[:, 8 * TOK:12 * TOK].rearrange("p (k m n) -> p k m n", k=2, m=2)
        h0 = shared[0:HALF, 12 * TOK:12 * TOK + 8 * D].rearrange("p (k m c d) -> p k m c d", k=2, m=2, c=2)
        prob = shared[0:HALF, 12 * TOK + 8 * D:16 * TOK + 8 * D].rearrange("p (c k) -> p c k", c=4)
        st1 = sb("st1", [HALF, 4, 6])
        mv1 = sb("mv1", [HALF, 4, 2])
        rs1 = sb("rs1", [HALF, 2, 4])
        xn = sb("xn", [HALF, 4, D])
        xnT_hi = sb("xnT_hi", [D, 2 * TOK], f32r)
        xnT_lo = sb("xnT_lo", [D, 2 * TOK], f32r)
        hid_hi, hid_lo = [p.rearrange("p (m n) -> p m n", m=2) for p in part[4:6]]
        kT = sb("kT", [DA, 2 * TOK])
        qT = sb("qT", [DA, 2 * TOK])
        emb = sb("emb", [HALF, 4, D])
        nmax = sb("nmax", [HALF, 4])
        rsum = sb("rsum", [HALF, 4])
        rinv = sb("rinv", [HALF, 4])
        probT = sb("probT", [HALF, 2, 2, TOK])
        h1 = sb("h1", [HALF, 2, 4, D])
        st2 = sb("st2", [HALF, 4, 6])
        mv2 = sb("mv2", [HALF, 4, 2])
        rs2 = sb("rs2", [HALF, 2, 4])
        xm = sb("xm", [HALF, 2, 4, D])
        xmT = sb("xmT", [D, 2 * TOK])
        lg_y = sb("lg_y", [128, E * COLS])
        lg = lg_y[0:HALF, :].rearrange("p (e c) -> p e c", e=E)

        prb = sb("prb", [HALF, E, COLS])
        numbers = sb("numbers", [128, 2 * GN])
        lgs = numbers[:, 0:GN]
        prs = numbers[:, GN:2 * GN]
        hi = sb("hi", [128, GN], u16)
        lo = sb("lo", [128, GN], u16)
        above = sb("above", [128, GN], u16)
        reach = sb("reach", [128, 3, GN], bf16)
        pmax = sb("pmax", [HALF, E])
        spread = sb("spread", [128, 128])
        ngmax = sb("ngmax", [128, E])
        ngown = sb("ngown", [128, 1])
        sum_p = sb("sum_p", [HALF, E])
        pinv = sb("pinv", [128, E])
        thr = sb("thr", [128, 2])
        thr_i = sb("thr_i", [128, 2], i32)
        thr_b = sb("thr_b", [128, 1], i32)
        limit = sb("limit", [HALF, E])
        cand = sb("cand", [128, 3])
        base = sb("base", [128, 3])
        lift = sb("lift", [128, 3])
        bit = sb("bit", [128, 1])
        low = sb("low", [128, 3])
        met = sb("met", [128, 3])
        gain = sb("gain", [128, 1])
        cnt = sb("cnt", [128, 3])
        rows_s = sb("rows_s", [128, 1])
        ngroup_s = sb("ngroup_s", [128, 128])
        cntg = sb("cntg", [HALF, E])
        scan = shared[0:HALF, 0:E * COLS].rearrange("p (e c) -> p e c", e=E)
        gteq = shared[0:HALF, E * COLS:2 * E * COLS].bitcast(bf16).rearrange("p (w e c) -> p w e c", w=2, e=E)
        gt, eq = gteq[:, 0], gteq[:, 1]
        need = sb("need", [HALF, E])
        zero_s = sb("zero_s", [HALF, COLS])
        tie = sb("tie", [HALF, E, COLS], bf16)
        sel = sb("sel", [HALF, E, COLS + 1], bf16)
        dsel = sb("dsel", [HALF, E, COLS], bf16)
        table = sb("table", [128, E, BLK, TW], bf16)
        tot = sb("tot", [128, BLK, E])
        first = sb("first", [128, BLK, E])
        begun = sb("begun", [128, 2, BLK, CAP], bf16)
        passed = sb("passed", [128, CH, HALF], bf16)
        slot = sb("slot", [128, 2, CH])
        place = sb("place", [128, 2, CH])
        row = sb("row", [128, E, CH], i32)

        g = xs[:].rearrange("p s k n -> p (s k n)")[:, 0:RING * CH * D].rearrange("p (e c d) -> p e c d", e=RING, c=CH)
        gT = numbers[:, 0:2 * CH * 128].rearrange("p (k c n) -> p k c n", k=2, c=CH)
        CT = CH * 128
        gT_hi, gT_lo = [parts[:, k * 2 * CT:(k + 1) * 2 * CT].rearrange("p (k c n) -> p k c n", k=2, c=CH)
                        for k in range(2)]
        w1_hi, w1_lo = [parts[:, 4 * CT + k * 2 * F:4 * CT + (k + 1) * 2 * F].rearrange("p (k f) -> p k f", k=2)
                        for k in range(2)]
        vexp = sb("vexp", [128, E, CH])
        val = sb("val", [128, E, CH])
        act1 = shared[:, :].rearrange("p (k f n) -> p k f n", k=2, f=FT)
        y = lg_y[:, :].rearrange("p (k c d) -> p k c d", k=4, c=4)

        B = [ctx.enter_context(nc.psum_tensor(f"bank{n}", [128, 512], f32)) for n in range(8)]

        s_w = sem("weights_loaded")
        s_w2 = sem("late_weights_loaded")
        s_const = sem("constants_made")
        s_wt = sem("patch_weights_loaded")
        s_wh = sem("weights_rounded")
        s_wl = sem("weights_split")
        s_ht0 = sem("class_column_set")
        s_x = [sem("x_loaded_0"), sem("x_loaded_1")]
        s_txt = [sem("txt_loaded_0"), sem("txt_loaded_1")]
        s_xh = sem("x_halves_rounded")
        s_xl = sem("x_halves_split")
        s_pj = [sem("proj_half_done"), sem("proj_done")]
        s_hT = sem("hT_ready")
        s_t0 = sem("h_turned")
        s_h0 = sem("h0_ready")
        s_st1 = sem("stats1_ready")
        s_mv1 = sem("meanvar1_ready")
        s_r1 = [sem("variance1_plus_eps"), sem("rstd1_ready")]
        s_xn = sem("xn_ready")
        s_t1 = sem("xn_turned")
        s_xnT = sem("xnT_rounded")
        s_xnl = sem("xnT_split")
        s_up = sem("up_done")
        s_ra = sem("relu_by_act")
        s_rh = sem("hid_rounded")
        s_rl = [sem("hid_0_split"), sem("hid_1_split")]
        s_kq = sem("kq_done")
        s_k = sem("kT_ready")
        s_q = sem("qT_ready")
        s_em = sem("emb_done")
        s_emb = sem("emb_ready")
        s_sc = sem("scores_done")
        s_nm = sem("nmax_ready")
        s_exp = sem("exp_done")
        s_ta = sem("prob_turned")
        s_pa = sem("probT_by_act")
        s_pd = sem("probT_by_dve")
        s_ri = sem("rinv_ready")
        s_o = sem("attention_done")
        s_h1 = sem("h1_ready")
        s_st2 = sem("stats2_ready")
        s_mv2 = sem("meanvar2_ready")
        s_r2 = [sem("variance2_plus_eps"), sem("rstd2_ready")]
        s_xm = sem("xm_ready")
        s_t2 = sem("xm_turned")
        s_xmT = sem("xmT_ready")
        s_l = sem("logits_done")
        s_lg = sem("logits_kept")
        s_out = [sem("rows_stored_0"), sem("rows_stored_1")]
        s_xs = [sem("xm_stored_0"), sem("xm_stored_1")]
        b_ls = sem("logits_in_scratch")
        b_ll = sem("logits_by_group")
        b_pm = sem("group_max_ready")
        b_sp = sem("spread_ready")
        b_sT = sem("spread_turned")
        b_ng = sem("ngmax_ready")
        b_no = sem("ngown_ready")
        b_ps = sem("prs_ready")
        b_ex = sem("prb_ready")
        b_su = sem("sum_done")
        b_pi = sem("pinv_ready")
        b_hl = sem("halves_ready")
        b_in = sem("search_set")
        b_ct = sem("counts_by_dve")
        b_cs = sem("counts_by_act")
        b_tt = sem("totals_done")
        b_nx = sem("bits_lowered")
        b_ba = sem("base_ready")
        b_kb = sem("gain_ready")
        b_ca = sem("candidates_ready")
        b_tu = sem("threshold_raised")
        b_lw = sem("lower_halves_steps")
        b_th = sem("threshold_steps")
        b_gt = sem("above_ready")
        b_ga = sem("above_counted")
        b_eq = sem("equal_ready")
        b_nd = sem("need_ready")
        b_rk = sem("tie_ranks_done")
        b_sc = sem("scan_steps")
        b_se = sem("sel_ready")
        b_tb = sem("table_done")
        b_ta = sem("table_kept")
        b_pf = sem("first_ranks_done")
        b_fr = sem("first_ranks_kept")
        b_be = sem("begun_ready")
        b_lo = sem("lookup_done")
        b_sl = sem("slot_ready")
        b_pl = sem("place_ready")
        b_ro = sem("rows_ready")
        c_g = [sem("gathered_0"), sem("gathered_1"), sem("gathered_2")]
        c_t = sem("gathered_turned")
        c_gT = sem("gT_ready")
        c_hr = sem("gT_and_w1_rounded")
        c_gp = sem("gT_and_w1_split")
        c_v = sem("val_logits_done")
        c_ve = sem("val_exp_done")
        c_va = sem("val_ready")
        c_up = sem("expert_up_done")
        c_ge = sem("gelu_done")
        c_dn = sem("expert_down_done")
        c_yb = sem("y_biased")
        c_y = sem("y_ready")
        c_sc = [sem("rows_added_0"), sem("rows_added_1")]

        NW = 11
        NL = 10

        def slot16(t, par):
            return 8 * (t - par) + 16

        def wait(eng, s, value):
            if not isinstance(value, int) or value > 0:
                eng.wait_ge(s, value)

        def steps(eng, step):
            for t in range(-2, 2):
                step(t, t % 2)
            with eng.Fori(2, PAIRS - 5, 2) as i:
                step(i, 0)
                step(i + 1, 1)
            for t in range(PAIRS - 4, PAIRS + 2):
                step(t, t % 2)

        def there(t):
            return not isinstance(t, int) or 0 <= t < PAIRS

        def product(pe, to, w_hi, w_lo, x_hi, x_lo, start, stop):
            pe.matmul(to, w_lo, x_hi, start=start, stop=False)
            pe.matmul(to, w_hi, x_hi, start=False, stop=False)
            return pe.matmul(to, w_hi, x_lo, start=False, stop=stop)

        def looked_up(e):
            return B[6:8] if e < LOOK else B[0:2]

        UP = [B[2], B[3], B[4], B[6]]
        block = ctx.enter_context(nc.Block())

        @block.sync
        def _(sp):
            def load_x(t, par):
                wait(sp, s_xl, 2 * t - 2)
                sp.dma_start(xs[:, par], x[t]).then_inc(s_x[par], 16)

            sp.dma_start(tokw_s[:], tok_w).then_inc(s_wt, 16)
            load_x(0, 0)
            load_x(1, 1)
            for dst, src in ((tokb_s, tok_b), (cls_s, cls), (pos_s, pos),
                             (ident_s, ident), (wup_s, w_up), (bup_s, b_up), (we2_s, w_e2),
                             (be2_s, b_e2), (wkq_s, w_kq), (bkq_s, b_kq), (wr_s, wr)):
                sp.dma_start(dst[:], src).then_inc(s_w, 16)

            def load_txt(t, par):
                wait(sp, s_h1, t - 1)
                sp.dma_start(h0[IMG_ROWS1:HALF, par, :, 1, :], txt[t]).then_inc(s_txt[par], 16)

            def store(t, par):
                wait(sp, s_h1, t + 1)
                sp.dma_start(pair_rows[t], h1[:, par]).then_inc(s_out[par], 16)

            for t in range(2):
                load_txt(t, t)
            for dst, src in ((upto_s, upto), (after_s, after), (before_s, before), (group_s, group),
                             (number_s, number), (rank_u, rank), (w1_s, w1), (b1_s, b1), (w2_s, w2),
                             (b2_s, b2)):
                sp.dma_start(dst[:], src).then_inc(s_w2, 16)
            def store_xm(t, par):
                wait(sp, s_xm, t + 1)
                sp.dma_start(xm_pairs[t], xm[:, par]).then_inc(s_xs[par], 16)

            def step(t, par):
                if there(t + 3):
                    load_x(t + 3, 1 - par)
                if there(t - 1):
                    store_xm(t - 1, 1 - par)
                store(t, par)
                if there(t + 2):
                    load_txt(t + 2, par)

            load_x(2, 0)
            for t in range(2):
                step(t, t)
            with sp.Fori(2, PAIRS - 5, 2) as i:
                step(i, 0)
                step(i + 1, 1)
            def to_scratch(part, cols):
                sp.dma_start(lg_dram[part].rearrange("e (p c) -> p e c", p=HALF), lg[:, :, cols]).then_inc(b_ls, 16)

            def by_group(part, cols):
                sp.wait_ge(b_ls, 16 * (part + 1))
                sp.dma_start(lgs[:, cols], lg_dram[part].rearrange("e (k n) -> (e k) n", k=GRP)).then_inc(b_ll, 16)

            for t in range(PAIRS - 4, PAIRS):
                step(t, t % 2)
                if t == PAIRS - 4:
                    sp.wait_ge(s_lg, PAIRS - LATE // 4)
                    to_scratch(0, slice(0, COLS - LATE))
                if t == PAIRS - 3:
                    by_group(0, slice(0, SPLIT))
            store_xm(PAIRS - 1, 1)
            sp.wait_ge(s_lg, PAIRS)
            to_scratch(1, slice(COLS - LATE, COLS))
            by_group(1, slice(SPLIT, GN))

        @block.tensor
        def _(pe):
            pe.wait_ge(s_wl, 1)

            def project(t, par, half):
                pe.wait_ge(s_xl, 2 * t + 1 + half)
                if half == 0:
                    wait(pe, s_hT, t - 1)
                    wait(pe, s_lg, t - 4)
                for k in range(3 * half, 3 * half + 3):
                    last = product(pe, B[par][:, 0:2 * PATCHES], tokw_hi[:, k, :], tokw_lo[:, k, :],
                                   xs_hi[:, k, :], xs_lo[:, k, :], k == 0, k == PK - 1)
                last.then_inc(s_pj[half], 1)

            def turn_h(t, par):
                pe.wait_ge(s_hT, t + 1)
                wait(pe, s_h1, t - 1)
                if isinstance(t, int) and t == 0:
                    pe.wait_ge(s_w, 16 * NW)
                    pe.wait_ge(s_wl, 2)
                    pe.wait_ge(s_ht0, 1)
                for m in range(2):
                    pe.transpose(B[5][0:HALF, (2 * m) * D:(2 * m + 1) * D], hT[:, par, m, 0:HALF],
                                 ident_s[:])
                    last = pe.transpose(B[5][0:IMG_ROWS1, (2 * m + 1) * D:(2 * m + 2) * D],
                                        hT[:, par, m, HALF:HALF + IMG_ROWS1], ident_s[:])
                last.then_inc(s_t0, 1)

            def turn_rows(bank, src, done):
                for c in range(4):
                    last = pe.transpose(bank[:, c * HALF:(c + 1) * HALF], src[:, c, :],
                                        ident_s[0:HALF, 0:HALF])
                last.then_inc(done, 1)

            def up(t):
                pe.wait_ge(s_xnl, t + 1)
                for m in range(4):
                    if m == 0:
                        wait(pe, s_pa, t)
                    if m == 1:
                        wait(pe, s_pd, t)
                    product(pe, UP[m][:, 0:2 * TOK], wup_hi[:, m, :], wup_lo[:, m, :], xnT_hi[:],
                            xnT_lo[:], True, True).then_inc(s_up, 1)

            def keys(t):
                for m in range(2):
                    pe.wait_ge(s_rl[m], t + 1)
                    last = product(pe, B[2][:, 0:2 * TOK], wkq_hi[:, m, :], wkq_lo[:, m, :],
                                   hid_hi[:, m, :], hid_lo[:, m, :], m == 0, m == 1)
                last.then_inc(s_kq, 1)

            def embed(t):
                pe.wait_ge(s_ra, 4 * t + 4)
                wait(pe, s_h1, t)
                for c in range(4):
                    for m in range(2):
                        last = pe.matmul(B[7][0:HALF, c * D:(c + 1) * D],
                                         hid[:, 2 + m, c * HALF:(c + 1) * HALF], we2_s[:, m, :],
                                         start=(m == 0), stop=(m == 1))
                last.then_inc(s_em, 1)

            def scores(t, m):
                if m == 0:
                    pe.wait_ge(s_k, t + 1)
                    pe.wait_ge(s_q, t + 1)
                    wait(pe, s_exp, 2 * t - 1)
                if m == 1:
                    pe.wait_ge(s_h0, t + 2 if not isinstance(t, int) else min(t + 2, PAIRS))
                for c in range(2):
                    at = m * TOK + c * HALF
                    last = pe.matmul(B[4 + m][0:HALF, c * TOK:(c + 1) * TOK],
                                     qT[:, at:at + HALF], kT[:, m * TOK:(m + 1) * TOK],
                                     start=True, stop=True)
                last.then_inc(s_sc, 1)

            def turn_xm(t, par):
                wait(pe, s_hT, t + 4 if not isinstance(t, int) else min(t + 4, PAIRS))
                wait(pe, s_lg, t - 1)
                pe.wait_ge(s_xm, t + 1)
                turn_rows(B[1 - par], xm[:, par], s_t2)

            def logits(t, par):
                pe.wait_ge(s_xmT, t + 1)
                for c in range(4):
                    last = pe.matmul(B[1 - par][0:HALF, 384 + c * E:384 + (c + 1) * E],
                                     xmT[:, c * HALF:(c + 1) * HALF], wr_s[:], start=True, stop=True)
                last.then_inc(s_l, 1)

            def turn_prob(t):
                for m in range(2):
                    pe.wait_ge(s_exp, 2 * t + 1 + m)
                    for kh in range(2):
                        for qh in range(2):
                            last = pe.transpose(
                                B[2 + m][0:HALF, kh * TOK + qh * HALF:kh * TOK + (qh + 1) * HALF],
                                prob[:, 2 * m + qh, kh * HALF:(kh + 1) * HALF],
                                ident_s[0:HALF, 0:HALF])
                    last.then_inc(s_ta, 1)

            def attend(t):
                pe.wait_ge(s_emb, t + 1)
                for m in range(2):
                    pe.wait_ge(s_pa if m == 0 else s_pd, t + 1)
                    for qh in range(2):
                        c = 2 * m + qh
                        for kh in range(2):
                            last = pe.matmul(B[7 - 2 * m][0:HALF, qh * D:(qh + 1) * D],
                                             probT[:, m, kh, qh * HALF:(qh + 1) * HALF],
                                             emb[:, 2 * m + kh, :], start=(kh == 0), stop=(kh == 1))
                    last.then_inc(s_o, 1)

            def step(t, par):
                if there(t):
                    keys(t)
                    embed(t)
                    scores(t, 0)
                    scores(t, 1)
                if there(t + 2):
                    project(t + 2, par, 1)
                if there(t - 2):
                    logits(t - 2, par)
                if there(t):
                    turn_prob(t)
                if there(t + 1):
                    pe.wait_ge(s_xn, t + 2)
                    turn_rows(B[6], xn, s_t1)
                if there(t):
                    attend(t)
                if there(t - 1):
                    turn_xm(t - 1, 1 - par)
                if there(t + 1):
                    up(t + 1)
                if there(t + 2):
                    turn_h(t + 2, par)
                if there(t + 3):
                    project(t + 3, 1 - par, 0)

            project(0, 0, 0)
            steps(pe, step)

            pe.wait_ge(s_const, 2)

            def turn_spread(n):
                pe.wait_ge(b_sp, n)
                rows = HALF if n == 1 else 128
                pe.transpose(B[n % 2][:, 0:rows], spread[0:rows, :], ident_s[0:rows, 0:rows]).then_inc(b_sT, 1)

            turn_spread(1)
            turn_spread(2)
            pe.matmul(B[3][:, 2:3], group_s[:], rows_s[:], start=True, stop=False)
            with pe.Fori(1, STEPS + 1) as i:
                pe.wait_ge(b_cs, i)
                pe.matmul(B[3][:, 2:3], ngroup_s[:], cnt[:, 2:3], start=False, stop=True)
                pe.wait_ge(b_ct, i)
                pe.matmul(B[3][:, 0:2], group_s[:], cnt[:, 0:2], start=True, stop=True).then_inc(b_tt, 1)
                pe.wait_ge(b_kb, i)
                pe.matmul(B[3][:, 2:3], group_s[:], rows_s[:], start=True, stop=False)
            pe.matmul(B[3][:, 2:3], ngroup_s[:], rows_s[:], start=False, stop=True)
            pe.wait_ge(b_ex, 1)
            pe.matmul(B[2][:, 0:E], ones_s[0:HALF, :], sum_p[:], start=True, stop=True).then_inc(b_su, 1)
            turn_spread(3)
            def tie_ranks(e):
                pe.matmul(B[e][0:HALF, 0:COLS], after_b[:], eq[:, e, :], start=True, stop=True)
                pe.matmul(B[e][0:HALF, COLS:2 * COLS], ones_b[:], eq[:, e, :], start=True,
                          stop=True).then_inc(b_rk, 1)

            pe.wait_ge(b_eq, 1)
            for e in RANKED[:-1]:
                tie_ranks(e)
            pe.wait_ge(b_gt, 1)
            pe.matmul(B[2][0:HALF, 0:E], ones_s[0:HALF, 0:HALF], cntg[:], start=True,
                      stop=True).then_inc(b_ga, 1)
            pe.wait_ge(b_nd, 1)
            tie_ranks(RANKED[-1])
            pe.wait_ge(b_se, 1)
            for w in range(2):
                for e in range(E):
                    for b in range(BLK):
                        at = 16 * w + b * E + e
                        last = pe.matmul(B[4][:, at:at + 1], sel[:, e, 1 - w + b * 128:1 - w + (b + 1) * 128],
                                         ones_b[:, 0:1], start=True, stop=True)
            last.then_inc(b_tb, 1)
            pe.wait_ge(b_se, 2)
            for e in range(E):
                for b in range(BLK):
                    at = (e % 2 * BLK + b) * HALF
                    last = pe.matmul(B[e // 2][:, at:at + HALF], dsel[:, e, b * 128:(b + 1) * 128],
                                     upto_b[:], start=True, stop=True)
            last.then_inc(b_tb, 1)
            pe.wait_ge(b_ta, 1)
            pe.matmul(B[5][:, 0:E], before_s[:], tot[:, 0, :], start=True, stop=True)
            pe.matmul(B[5][:, E:2 * E], before_s[:], tot[:, 1, :], start=True, stop=False)
            pe.matmul(B[5][:, E:2 * E], ones_s[:], tot[:, 0, :], start=False, stop=True).then_inc(b_pf, 1)

            def lookup(e):
                pe.wait_ge(b_ta, 2 + e // 2)
                pe.wait_ge(b_be, e + 1)
                if e >= 1:
                    pe.wait_ge(b_ro, e)
                if e >= LOOK:
                    pe.wait_ge(c_ve, e - LOOK + 2)
                    pe.wait_ge(c_gT, 2 * (e - LOOK + 2))
                for c in range(CH):
                    for b in range(BLK):
                        last = pe.matmul(looked_up(e)[c // 4][:, (c % 4) * 96:(c % 4) * 96 + TW],
                                         begun[:, e % 2, b, c * 128:(c + 1) * 128], table[:, e, b, :],
                                         start=(b == 0), stop=(b == BLK - 1))
                last.then_inc(b_lo, 1)

            for e in range(LOOK):
                lookup(e)

            def turn_gathered(e):
                pe.wait_ge(c_g[e % RING], 16 * CH * (e // RING + 1))
                if e == 0:
                    pe.wait_ge(b_ta, 1 + E // 2)
                else:
                    pe.wait_ge(b_ro, min(e + LOOK - 1, E))
                    pe.wait_ge(c_gT, 2 * e)
                    pe.wait_ge(c_ve, e)
                for q in range(2):
                    for c in range(4):
                        last = pe.transpose(B[q][:, c * 128:(c + 1) * 128], g[:, e % RING, 4 * q + c, :],
                                            ident_s[:])
                    last.then_inc(c_t, 1)

            def val_logits(e):
                pe.wait_ge(c_gT, 2 * e + 2)
                for c in range(CH):
                    last = pe.matmul(B[0][:, c:c + 1], gT[:, e % 2, c, :], wr_s[:, e:e + 1],
                                     start=True, stop=True)
                last.then_inc(c_v, 1)

            def expert_up(n):
                e, q = n // 2, n % 2
                pe.wait_ge(c_gp, e + 1)
                for f in range(FT):
                    k = n * FT + f
                    cols = slice(f * 128, (f + 1) * 128)
                    if k >= 4:
                        pe.wait_ge(c_ge, k - 3)
                    product(pe, B[2 + k % 4][:, :], w1_hi[:, e % 2, cols], w1_lo[:, e % 2, cols],
                            gT_hi[:, e % 2, 4 * q:4 * q + 4, :], gT_lo[:, e % 2, 4 * q:4 * q + 4, :],
                            True, True).then_inc(c_up, 1)

            def expert_down(n):
                e = n // 2
                pe.wait_ge(c_ge, FT * (n + 1))
                if n >= 2:
                    pe.wait_ge(c_yb, n - 1)
                else:
                    pe.wait_ge(b_ro, LOOK)
                for c in range(4):
                    for f in range(FT):
                        last = pe.matmul(B[6 + n % 2][:, c * D:(c + 1) * D],
                                         act1[:, n % 2, f, c * 128:(c + 1) * 128], w2_s[:, e, f, :],
                                         start=(f == 0), stop=(f == FT - 1))
                last.then_inc(c_dn, 1)

            pe.wait_ge(s_w2, 16 * NL)
            turn_gathered(0)
            val_logits(0)
            for n in range(2 * E):
                ahead = n // 2 + 1 if n % 2 == 0 and n // 2 + 1 < E else None
                expert_up(n)
                if ahead is not None:
                    turn_gathered(ahead)
                if n >= 1:
                    expert_down(n - 1)
                if ahead is not None:
                    val_logits(ahead)
                if n % 2 == 1 and n // 2 + LOOK < E:
                    lookup(n // 2 + LOOK)
            expert_down(2 * E - 1)

        @block.scalar
        def _(act):
            def round_x(t, par, half):
                act.wait_ge(s_x[par], slot16(t, par))
                wait(act, s_pj[half], t)
                part = slice(3 * half, 3 * half + 3)
                act.copy(xs_hi[:, part, :], xs[:, par, part, :]).then_inc(s_xh, 1)

            def keep_hT(t, par):
                act.wait_ge(s_pj[1], t + 1)
                wait(act, s_t0, t - 1)
                act.activation(hT[:, par, :, 1:1 + PATCHES],
                               B[par][:, 0:2 * PATCHES].rearrange("p (m n) -> p m n", m=2),
                               ACT.Identity, bias=tokb_s[:]).then_inc(s_hT, 1)

            def relus(t):
                for m in range(4):
                    act.wait_ge(s_up, 4 * t + 1 + m)
                    wait(act, s_rl[m] if m < 2 else s_em, t)
                    act.activation(hid[:, m, :], UP[m][:, 0:2 * TOK], ACT.Relu,
                                   bias=bup_s[:, m:m + 1]).then_inc(s_ra, 1)
                    if m < 2:
                        act.wait_ge(s_ra, 4 * t + 1 + m)
                        wait(act, s_kq, t)
                        act.copy(hid_hi[:, m, :], hid[:, m, :]).then_inc(s_rh, 1)

            def keep_k(t):
                act.wait_ge(s_kq, t + 1)
                wait(act, s_sc, 2 * t)
                act.activation(kT[:], B[2][0:DA, 0:2 * TOK], ACT.Identity,
                               bias=bkq_s[0:DA, :]).then_inc(s_k, 1)

            def keep_xmT(t, par):
                act.wait_ge(s_t2, t + 1)
                wait(act, s_l, t)
                act.copy(xmT[:], B[1 - par][:, 0:2 * TOK]).then_inc(s_xmT, 1)

            def keep_logits(t, par):
                act.wait_ge(s_l, t + 1)
                act.copy(lg[:, :, bass.ds(4 * t, 4)].rearrange("p e c -> p c e"),
                         B[1 - par][0:HALF, 384:384 + 4 * E].rearrange("p (c e) -> p c e", c=4)
                         ).then_inc(s_lg, 1)

            def exps(t):
                for m in range(2):
                    act.wait_ge(s_nm, 2 * t + 1 + m)
                    if m == 0:
                        wait(act, s_ta, 2 * t)
                        wait(act, s_ri, t)
                    for c in range(2):
                        k = 2 * m + c
                        last = act.activation(prob[:, k, :], B[4 + m][0:HALF, c * TOK:(c + 1) * TOK],
                                              ACT.Exp, bias=nmax[:, k:k + 1],
                                              accum_out=rsum[:, k:k + 1])
                    last.then_inc(s_exp, 1)

            def keep_probT(t):
                act.wait_ge(s_ta, 2 * t + 1)
                wait(act, s_o, 2 * t)
                act.copy(probT[:, 0, :, :], B[2][0:HALF, 0:2 * TOK].rearrange("p (k q) -> p k q", k=2)
                         ).then_inc(s_pa, 1)

            def keep_xnT(t):
                act.wait_ge(s_t1, t + 1)
                wait(act, s_up, 4 * t)
                act.copy(xnT_hi[:], B[6][:, 0:2 * TOK]).then_inc(s_xnT, 1)

            def step(t, par):
                if there(t):
                    keep_k(t)
                if there(t + 3):
                    round_x(t + 3, 1 - par, 0)
                if there(t):
                    exps(t)
                    keep_probT(t)
                if there(t - 2):
                    keep_logits(t - 2, par)
                if there(t + 2):
                    keep_hT(t + 2, par)
                if there(t + 1):
                    keep_xnT(t + 1)
                if there(t + 3):
                    round_x(t + 3, 1 - par, 1)
                if there(t - 1):
                    keep_xmT(t - 1, 1 - par)
                if there(t + 1):
                    relus(t + 1)

            round_x(0, 0, 0)
            round_x(0, 0, 1)
            act.wait_ge(s_w, 16 * NW)
            for par in range(2):
                for m in range(2):
                    last = act.copy(hT[:, par, m, 0:1], cls_s[:])
            last.then_inc(s_ht0, 1)
            steps(act, step)

            act.wait_ge(b_no, 1)
            act.wait_ge(b_ll, 32)
            act.activation(prs[:], lgs[:], ACT.Exp, bias=ngown[:]).then_inc(b_ps, 1)

            def count(numbers):
                act.activation(reach[:, 2, :], numbers, ACT.Sign, bias=cand[:, 2:3], scale=-1.0,
                               accum_out=cnt[:, 2:3]).then_inc(b_cs, 1)

            act.wait_ge(b_in, 1)
            act.wait_ge(b_hl, 1)
            count(hi[:])
            with act.Fori(1, HI_STEPS) as i:
                act.wait_ge(b_ca, i)
                count(hi[:])
            act.wait_ge(b_ng, 1)
            for e in range(E):
                last = act.activation(prb[:, e, :], lg[:, e, :], ACT.Exp, bias=ngmax[0:HALF, e:e + 1],
                                      accum_out=sum_p[:, e:e + 1])
            last.then_inc(b_ex, 1)
            act.wait_ge(b_in, 2)
            act.wait_ge(b_lw, 2)
            count(lo[:])
            with act.Fori(HI_STEPS + 1, STEPS) as i:
                act.wait_ge(b_ca, i)
                count(lo[:])

            def keep_gT(e):
                if e >= 2:
                    act.wait_ge(c_gp, e - 1)
                    act.wait_ge(c_v, e - 1)
                for q in range(2):
                    act.wait_ge(c_t, 2 * e + q + 1)
                    act.copy(gT[:, e % 2, 4 * q:4 * q + 4, :], B[q][:].rearrange("p (c n) -> p c n", c=4)
                             ).then_inc(c_gT, 1)
                act.wait_ge(c_v, e + 1)
                act.activation(vexp[:, e, :], B[0][:, 0:CH], ACT.Exp, bias=ngmax[:, e:e + 1]
                               ).then_inc(c_ve, 1)

            act.wait_ge(s_w2, 16 * NL)
            keep_gT(0)
            for n in range(2 * E):
                if n >= 2:
                    act.wait_ge(c_dn, n - 1)
                for f in range(FT):
                    k = n * FT + f
                    act.wait_ge(c_up, k + 1)
                    act.activation(act1[:, n % 2, f, :], B[2 + k % 4][:, :], ACT.Gelu,
                                   bias=b1_s[:, n // 2, f:f + 1]).then_inc(c_ge, 1)
                if n % 2 == 0 and n // 2 + 1 < E:
                    keep_gT(n // 2 + 1)

        @block.vector
        def _(dve):
            dve.memset(ones_s[:], 1.0)
            dve.memset(ones_b[:], 1.0)
            dve.memset(half_s[:], -0.5)
            dve.memset(eps_s[:], EPS)
            dve.memset(zero_s[:], 0.0).then_inc(s_const, 1)
            dve.wait_ge(s_wt, 16)
            dve.tensor_copy(tokw_hi[:], tokw_s[:]).then_inc(s_wh, 1)
            dve.wait_ge(s_wh, 1)
            dve.tensor_tensor(tokw_lo[:], tokw_s[:], tokw_hi[:].bitcast(f32), ALU.subtract).then_inc(s_wl, 1)
            dve.wait_ge(s_w, 16 * NW)
            split = ((wup_s, wup_hi, wup_lo), (wkq_s, wkq_hi, wkq_lo))
            for w, w_hi, w_lo in split:
                last = dve.tensor_copy(w_hi[:], w[:])
            last.then_inc(s_wh, 1)
            dve.wait_ge(s_wh, 2)
            for w, w_hi, w_lo in split:
                last = dve.tensor_tensor(w_lo[:], w[:], w_hi[:].bitcast(f32), ALU.subtract)
            last.then_inc(s_wl, 1)

            def split_hid1(t):
                dve.wait_ge(s_rh, 2 * t + 2)
                dve.tensor_tensor(hid_lo[:, 1, :], hid[:, 1, :], hid_hi[:, 1, :].bitcast(f32),
                                  ALU.subtract).then_inc(s_rl[1], 1)

            def split_xnT(t):
                dve.wait_ge(s_xnT, t + 1)
                dve.tensor_tensor(xnT_lo[:], B[6][:, 0:2 * TOK], xnT_hi[:].bitcast(f32),
                                  ALU.subtract).then_inc(s_xnl, 1)

            def keep_q(t):
                dve.wait_ge(s_kq, t + 1)
                wait(dve, s_sc, 2 * t)
                dve.tensor_scalar(qT[:], B[2][DA:2 * DA, 0:2 * TOK], bkq_s[DA:2 * DA, :], None,
                                  ALU.add).then_inc(s_q, 1)

            def keep_emb(t):
                dve.wait_ge(s_em, t + 1)
                dve.tensor_tensor(emb[:], B[7][0:HALF, :].rearrange("p (c d) -> p c d", c=4),
                                  be2_s[0:HALF, :].unsqueeze(1).to_broadcast([HALF, 4, D]),
                                  ALU.add).then_inc(s_emb, 1)

            def maxima(t, m):
                dve.wait_ge(s_sc, 2 * t + 1 + m)
                wait(dve, s_exp, 2 * t)
                dve.tensor_reduce(nmax[:, 2 * m:2 * m + 2],
                                  B[4 + m][0:HALF, 0:2 * TOK].rearrange("p (c k) -> p c k", c=2),
                                  AX.X, ALU.max, negate=True).then_inc(s_nm, 1)

            def stats(rows, st, s_st):
                for c in range(4):
                    last = dve.bn_stats(st[:, c, :], rows[:, c, :])
                last.then_inc(s_st, 1)

            def stats_there(t, s_st, used):
                wait(dve, used, t)
                dve.wait_ge(s_st, t + 1)

            def mean_variance(st, mv, s_mv):
                for c in range(4):
                    last = dve.bn_aggr(mv[:, c, :], st[:, c, :])
                last.then_inc(s_mv, 1)

            def normalise(t, n, rows, mv, rs, outs, s_r, done):
                dve.wait_ge(s_const, 1)
                dve.wait_ge(s_r, t + 1)
                for c in range(n):
                    last = dve.tensor_scalar(outs[:, c, :], rows[:, c, :], mv[:, c, 0:1],
                                             rs[:, 1, c:c + 1], ALU.subtract, ALU.mult)
                last.then_inc(done, 1)

            def normalise_h0(t, par):
                wait(dve, s_t1, t)
                normalise(t, 4, h0[:, par].rearrange("p m c d -> p (m c) d"), mv1, rs1, xn, s_r1[1], s_xn)

            def normalise_h1(t, par):
                wait(dve, s_t2, t - 1)
                wait(dve, s_xs[par], slot16(t - 2, par))
                normalise(t, 4, h1[:, par], mv2, rs2, xm[:, par], s_r2[1], s_xm)

            def keep_h0(t, par):
                dve.wait_ge(s_t0, t + 1)
                turned = B[5][:, :].rearrange("p (m c d) -> p m c d", m=2, c=2)
                dve.tensor_scalar(h0[:, par, :, 0, :], turned[0:HALF, :, 0, :], pos_s[:, 0:1], None,
                                  ALU.add)
                dve.tensor_scalar(h0[0:IMG_ROWS1, par, :, 1, :], turned[0:IMG_ROWS1, :, 1, :],
                                  pos_s[0:IMG_ROWS1, 1:2], None, ALU.add).then_inc(s_h0, 1)

            def stats_h0(t, par):
                dve.wait_ge(s_h0, t + 1)
                dve.wait_ge(s_txt[par], slot16(t, par))
                stats(h0[:, par].rearrange("p m c d -> p (m c) d"), st1, s_st1)

            def keep_probT(t):
                dve.wait_ge(s_ta, 2 * t + 2)
                wait(dve, s_o, 2 * t)
                dve.tensor_copy(probT[:, 1, :, :],
                                B[3][0:HALF, 0:2 * TOK].rearrange("p (k q) -> p k q", k=2)
                                ).then_inc(s_pd, 1)
                dve.reciprocal(rinv[:], rsum[:]).then_inc(s_ri, 1)

            def residual(t, par):
                dve.wait_ge(s_ri, t + 1)
                wait(dve, s_out[par], slot16(t - 2, par))
                wait(dve, s_xm, t - 1)
                for c in range(4):
                    if c % 2 == 0:
                        dve.wait_ge(s_o, 2 * t + 1 + c // 2)
                    last = dve.scalar_tensor_tensor(out=h1[:, par, c, :], 
                                                    in0=B[7 - c // 2 * 2][0:HALF, c % 2 * D:(c % 2 + 1) * D],
                                                    scalar=rinv[:, c:c + 1], in1=h0[:, par, c // 2, c % 2, :],
                                                    op0=ALU.mult, op1=ALU.add)
                last.then_inc(s_h1, 1)
                dve.wait_ge(s_h1, t + 1)
                stats(h1[:, par], st2, s_st2)
                dve.wait_ge(s_const, 1)
                stats_there(t, s_st2, s_xm)
                mean_variance(st2, mv2, s_mv2)

            def step(t, par):
                if there(t + 1):
                    stats_there(t + 1, s_st1, s_xn)
                if there(t):
                    keep_q(t)
                if there(t + 1):
                    mean_variance(st1, mv1, s_mv1)
                if there(t):
                    maxima(t, 0)
                    maxima(t, 1)
                if there(t + 1):
                    normalise_h0(t + 1, 1 - par)
                if there(t):
                    keep_emb(t)
                    keep_probT(t)
                if there(t - 1):
                    normalise_h1(t - 1, 1 - par)
                if there(t + 1):
                    split_xnT(t + 1)
                if there(t):
                    residual(t, par)
                if there(t + 1):
                    split_hid1(t + 1)
                if there(t + 2):
                    keep_h0(t + 2, par)
                    stats_h0(t + 2, par)

            steps(dve, step)

            dve.wait_ge(s_w2, 16 * NL)
            dve.tensor_copy(upto_b[:], upto_s[:])
            dve.tensor_copy(after_b[:], after_s[:])
            dve.memset(sel[:, :, 0:1], 0.0)
            dve.memset(low[:, 0:2], 0.0)
            dve.memset(low[:, 2:3], -0.5)
            dve.memset(rows_s[:], GN / 2)
            dve.tensor_scalar(ngroup_s[:], group_s[:], -0.5, None, ALU.mult).then_inc(s_const, 1)
            dve.wait_ge(s_const, 2)
            dve.wait_ge(s_lg, PAIRS)
            dve.tensor_reduce(pmax[:], lg[:], AX.X, ALU.max).then_inc(b_pm, 1)
            dve.wait_ge(b_pm, 1)
            dve.tensor_copy(spread[0:HALF, :].rearrange("p (e k) -> p e k", e=E),
                            pmax[:].unsqueeze(2).to_broadcast([HALF, E, GRP])).then_inc(b_sp, 1)
            dve.wait_ge(b_sT, 1)
            dve.tensor_reduce(ngown[:], B[1][:, 0:HALF], AX.X, ALU.max, negate=True).then_inc(b_no, 1)
            dve.wait_ge(b_no, 1)
            dve.tensor_copy(spread[:], ngown[:].to_broadcast([128, 128])).then_inc(b_sp, 1)
            dve.wait_ge(b_sT, 2)
            dve.tensor_copy(ngmax[:], B[0][:, 0:128:GRP]).then_inc(b_ng, 1)

            def start_search(bits):
                step = 1 << (bits - 2)
                dve.memset(bit[:], float(step))
                for k in range(3):
                    dve.memset(lift[:, k:k + 1], (k + 1) * step / 4)
                    dve.memset(base[:, k:k + 1], (k + 1) * step / 4 - (k == 2) / 2)
                    last = dve.memset(cand[:, k:k + 1], (k + 1) * step - (k == 2) / 2)
                last.then_inc(b_in, 1)

            def count(numbers):
                for k in range(2):
                    last = dve.tensor_scalar(reach[:, k, :], numbers, cand[:, k:k + 1], None, ALU.is_ge,
                                             ALU.add, accum_out=cnt[:, k:k + 1])
                last.then_inc(b_ct, 1)

            def search(numbers, t, first, last):
                def step(i, ends):
                    dve.wait_ge(b_tt, i)
                    dve.tensor_scalar(met[:], B[3][:, 0:3], float(CAP), None, ALU.is_ge, ALU.add,
                                      accum_out=gain[:]).then_inc(b_kb, 1)
                    dve.wait_ge(b_kb, i)
                    dve.scalar_tensor_tensor(out=cand[:], in0=gain[:].to_broadcast([128, 3]), scalar=bit[:],
                                             in1=base[:], op0=ALU.mult, op1=ALU.add).then_inc(b_ca, 1)
                    dve.scalar_tensor_tensor(out=t, in0=gain[:], scalar=bit[:], in1=t, op0=ALU.mult,
                                             op1=ALU.add).then_inc(b_tu, 1)
                    dve.wait_ge(b_ca, i)
                    if not ends:
                        count(numbers)
                    dve.wait_ge(b_tu, i)
                    dve.tensor_scalar(bit[:], bit[:], 0.25, None, ALU.mult)
                    dve.tensor_scalar(lift[:], lift[:], 0.25, None, ALU.mult).then_inc(b_nx, 1)
                    dve.wait_ge(b_nx, i)
                    dve.scalar_tensor_tensor(out=base[:], in0=lift[:], scalar=t, in1=low[:], op0=ALU.add,
                                             op1=ALU.add).then_inc(b_ba, 1)
                    dve.wait_ge(b_ba, i)

                count(numbers)
                with dve.Fori(first, last) as i:
                    step(i, False)
                step(last, True)

            dve.memset(thr[:], 0.0)
            start_search(HI_BITS)
            dve.wait_ge(b_in, 1)
            dve.wait_ge(b_ps, 1)
            halves = prs[:].bitcast(u16).rearrange("p (n h) -> p h n", h=2)
            dve.tensor_copy(hi[:], halves[:, 1, :]).then_inc(b_hl, 1)
            dve.wait_ge(b_hl, 1)
            search(hi[:], thr[:, 0:1], 1, HI_STEPS)
            start_search(LO_BITS)
            dve.tensor_scalar(above[:], hi[:], thr[:, 0:1], 65535.0, ALU.is_gt, ALU.mult)
            dve.scalar_tensor_tensor(out=lo[:], in0=hi[:], scalar=thr[:, 0:1], in1=halves[:, 0, :],
                                     op0=ALU.is_equal, op1=ALU.mult).then_inc(b_lw, 1)
            dve.wait_ge(b_lw, 1)
            dve.wait_ge(b_in, 2)
            dve.tensor_tensor(lo[:], lo[:], above[:], ALU.max).then_inc(b_lw, 1)
            dve.wait_ge(b_lw, 2)
            search(lo[:], thr[:, 1:2], HI_STEPS + 1, STEPS)
            dve.tensor_copy(thr_i[:], thr[:]).then_inc(b_th, 1)
            dve.wait_ge(b_th, 1)
            dve.scalar_tensor_tensor(out=thr_b[:], in0=thr_i[:, 0:1], scalar=16, in1=thr_i[:, 1:2],
                                     op0=ALU.logical_shift_left, op1=ALU.bitwise_or).then_inc(b_th, 1)
            dve.wait_ge(b_th, 2)
            dve.tensor_copy(spread[:].bitcast(i32), thr_b[:].to_broadcast([128, 128])).then_inc(b_sp, 1)
            dve.wait_ge(b_su, 1)
            dve.reciprocal(pinv[:], B[2][:, 0:E]).then_inc(b_pi, 1)
            dve.wait_ge(b_sT, 3)
            dve.tensor_copy(limit[:].bitcast(i32), B[1][0:HALF, 0:128:GRP].bitcast(i32)).then_inc(b_th, 1)
            dve.wait_ge(b_th, 3)
            dve.wait_ge(b_pi, 1)

            for e in range(E):
                last = dve.tensor_scalar(eq[:, e, :], prb[:, e, :], limit[:, e:e + 1], None, ALU.is_equal)
            last.then_inc(b_eq, 1)
            for e in range(E):
                last = dve.tensor_scalar(gt[:, e, :], prb[:, e, :], limit[:, e:e + 1], None, ALU.is_gt,
                                         ALU.add, accum_out=cntg[:, e:e + 1])
            last.then_inc(b_gt, 1)
            for k, e in enumerate(RANKED):
                if k == E - 1:
                    dve.wait_ge(b_ga, 1)
                    dve.tensor_scalar(need[:], B[2][0:HALF, 0:E], -1.0, float(CAP - BIG), ALU.mult,
                                      ALU.add).then_inc(b_nd, 1)
                dve.wait_ge(b_rk, k + 1)
                last = dve.tensor_tensor_scan(scan[:, e, :], zero_s[:], B[e][0:HALF, COLS:2 * COLS], 0.0,
                                              ALU.add, ALU.add)
            last.then_inc(b_sc, 1)
            dve.wait_ge(b_sc, 1)
            dve.wait_ge(b_nd, 1)
            for e in range(E):
                last = dve.scalar_tensor_tensor(out=tie[:, e, :], in0=scan[:, e, :], scalar=need[:, e:e + 1],
                                                in1=B[e][0:HALF, 0:COLS], op0=ALU.subtract, op1=ALU.is_le)
            last.then_inc(b_sc, 1)
            dve.wait_ge(b_sc, 2)
            dve.wait_ge(b_gt, 1)
            dve.tensor_tensor(sel[:, :, 1:], tie[:], gt[:], ALU.add).then_inc(b_se, 1)
            dve.wait_ge(b_se, 1)
            dve.tensor_tensor(dsel[:], sel[:, :, 1:], sel[:, :, 0:COLS], ALU.subtract).then_inc(b_se, 1)
            dve.wait_ge(b_tb, 1)
            dve.tensor_copy(tot[:], B[4][:, 0:2 * E].rearrange("p (b e) -> p b e", b=BLK)).then_inc(b_ta, 1)
            dve.tensor_copy(table[:, :, :, HALF], B[4][:, 2 * E:4 * E].rearrange("p (b e) -> p e b", b=BLK))
            dve.tensor_copy(table[:, :, :, HALF + 1],
                            number_s[:, CH:CH + BLK].unsqueeze(1).to_broadcast([128, E, BLK]))
            dve.wait_ge(b_tb, 2)

            def keep_table(k):
                dve.tensor_copy(table[:, 2 * k:2 * k + 2, :, 0:HALF],
                                B[k][:, 0:4 * HALF].rearrange("p (e b n) -> p e b n", e=2, b=BLK)
                                ).then_inc(b_ta, 1)

            keep_table(0)
            dve.wait_ge(b_pf, 1)
            dve.tensor_copy(first[:], B[5][:, 0:2 * E].rearrange("p (b e) -> p b e", b=BLK)).then_inc(b_fr, 1)
            dve.wait_ge(b_fr, 1)

            def columns_begun(e):
                if e >= 2:
                    dve.wait_ge(b_lo, e - 1)
                for b in range(BLK):
                    last = dve.tensor_scalar(begun[:, e % 2, b, :], rank_u[:], first[:, b, e:e + 1], None,
                                             ALU.is_ge)
                last.then_inc(b_be, 1)

            def find_rows(e):
                k = e % 2
                dve.wait_ge(b_lo, e + 1)
                for q in range(2):
                    looked = looked_up(e)[q][:, 0:384].rearrange("p (c n) -> p c n", c=4)
                    last = dve.tensor_tensor(slot[:, k, 4 * q:4 * q + 4], number_s[:, 4 * q:4 * q + 4],
                                             looked[:, :, HALF], ALU.subtract)
                last.then_inc(b_sl, 1)
                dve.wait_ge(b_sl, e + 1)
                for c in range(CH):
                    at = (c % 4) * 96
                    last = dve.tensor_scalar(passed[:, c, :], looked_up(e)[c // 4][:, at:at + HALF],
                                             slot[:, k, c:c + 1], None, ALU.is_le, ALU.add,
                                             accum_out=place[:, k, c:c + 1])
                last.then_inc(b_pl, 1)
                dve.wait_ge(b_pl, e + 1)
                for q in range(2):
                    looked = looked_up(e)[q][:, 0:384].rearrange("p (c n) -> p c n", c=4)
                    last = dve.scalar_tensor_tensor(out=row[:, e, 4 * q:4 * q + 4],
                                                    in0=looked[:, :, HALF + 1], scalar=float(HALF),
                                                    in1=place[:, k, 4 * q:4 * q + 4], op0=ALU.mult, op1=ALU.add)
                last.then_inc(b_ro, 1)

            columns_begun(0)
            for e in range(LOOK):
                columns_begun(e + 1)
                find_rows(e)
                if e + 1 < E // 2:
                    keep_table(e + 1)

            def split_inputs(e):
                if e >= 2:
                    dve.wait_ge(c_up, 2 * FT * (e - 1))
                dve.tensor_copy(w1_hi[:, e % 2, :], w1_s[:, e, :])
                dve.wait_ge(c_gT, 2 * e + 2)
                dve.tensor_copy(gT_hi[:, e % 2], gT[:, e % 2]).then_inc(c_hr, 1)
                dve.wait_ge(c_hr, e + 1)
                dve.tensor_tensor(w1_lo[:, e % 2, :], w1_s[:, e, :], w1_hi[:, e % 2, :].bitcast(f32), ALU.subtract)
                dve.tensor_tensor(gT_lo[:, e % 2], gT[:, e % 2], gT_hi[:, e % 2].bitcast(f32),
                                  ALU.subtract).then_inc(c_gp, 1)

            def values(e):
                dve.wait_ge(c_ve, e + 1)
                dve.tensor_scalar(val[:, e, :], vexp[:, e, :], pinv[:, e:e + 1], None, ALU.mult
                                  ).then_inc(c_va, 1)

            def weigh(n):
                e, q = n // 2, n % 2
                dve.wait_ge(c_dn, n + 1)
                if n >= 4:
                    dve.wait_ge(c_sc[e % 2], 16 * CH * (e // 2))
                dve.tensor_tensor(y[:, n % 4], B[6 + n % 2][:].rearrange("p (c d) -> p c d", c=4),
                                  b2_s[:, e, :].unsqueeze(1).to_broadcast([128, 4, D]),
                                  ALU.add).then_inc(c_yb, 1)
                dve.wait_ge(c_yb, n + 1)
                dve.wait_ge(c_va, e + 1)
                dve.tensor_tensor(y[:, n % 4], y[:, n % 4],
                                  val[:, e, 4 * q:4 * q + 4].unsqueeze(2).to_broadcast([128, 4, D]),
                                  ALU.mult).then_inc(c_y, 1)

            split_inputs(0)
            values(0)
            for n in range(2 * E):
                if n >= 1:
                    weigh(n - 1)
                if n % 2 == 0 and n // 2 + 1 < E:
                    split_inputs(n // 2 + 1)
                    values(n // 2 + 1)
                if n % 2 == 1 and n // 2 + LOOK < E:
                    find_rows(n // 2 + LOOK)
                    if n // 2 + LOOK + 1 < E:
                        columns_begun(n // 2 + LOOK + 1)
            weigh(2 * E - 1)

        @block.gpsimd
        def _(pool):
            pool.wait_ge(s_const, 1)

            def split_x(t, par, half):
                pool.wait_ge(s_xh, 2 * t + 1 + half)
                part = slice(3 * half, 3 * half + 3)
                pool.tensor_tensor(xs_lo[:, part, :], xs[:, par, part, :], xs_hi[:, part, :].bitcast(f32),
                                   ALU.subtract).then_inc(s_xl, 1)

            def split_hid0(t):
                pool.wait_ge(s_rh, 2 * t + 1)
                pool.tensor_tensor(hid_lo[:, 0, :], hid[:, 0, :], hid_hi[:, 0, :].bitcast(f32),
                                   ALU.subtract).then_inc(s_rl[0], 1)

            def rstd(t, n, mv, rs, s_r):
                pool.tensor_tensor(rs[:, 0, :], mv[:, :, 1], eps_s[0:rs.shape[0], 0:n], ALU.add).then_inc(s_r[0], 1)
                pool.wait_ge(s_r[0], t + 1)
                pool.tensor_tensor(rs[:, 1, :], rs[:, 0, :], half_s[0:rs.shape[0], 0:n], ALU.pow).then_inc(s_r[1], 1)

            def step(t, par):
                if there(t + 1):
                    pool.wait_ge(s_mv1, t + 2)
                    wait(pool, s_xn, t + 1)
                    rstd(t + 1, 4, mv1, rs1, s_r1)
                if there(t + 3):
                    split_x(t + 3, 1 - par, 0)
                    split_x(t + 3, 1 - par, 1)
                if there(t + 1):
                    split_hid0(t + 1)
                if there(t):
                    pool.wait_ge(s_mv2, t + 1)
                    wait(pool, s_xm, t)
                    rstd(t, 4, mv2, rs2, s_r2)
            split_x(0, 0, 0)
            split_x(0, 0, 1)
            steps(pool, step)

            for par in range(2):
                pool.wait_ge(s_xs[par], 16 * (PAIRS // 2))
                pool.wait_ge(s_out[par], 16 * (PAIRS // 2))

            def gather(e):
                pool.wait_ge(b_ro, e + 1)
                if e >= RING:
                    pool.wait_ge(c_t, 2 * (e - RING) + 2)
                for c in range(CH):
                    pool.indirect_dma_start(out=g[:, e % RING, c, :], out_offset=None, in_=xm_dram,
                                            in_offset=bass.IndirectOffsetOnAxis(ap=row[:, e, c:c + 1], axis=0)
                                            ).then_inc(c_g[e % RING], 16)

            def add_rows(n):
                e, q = n // 2, n % 2
                pool.wait_ge(c_y, n + 1)
                if q == 0 and e >= 1:
                    pool.wait_ge(c_sc[(e - 1) % 2], 16 * CH * ((e - 1) // 2 + 1))
                for c in range(4):
                    pool.indirect_dma_start(out=rows_dram, in_=y[:, n % 4, c, :], in_offset=None,
                                            out_offset=bass.IndirectOffsetOnAxis(
                                                ap=row[:, e, 4 * q + c:4 * q + c + 1], axis=0),
                                            compute_op=ALU.add).then_inc(c_sc[e % 2], 16)

            for e in range(RING):
                gather(e)
            for e in range(E):
                if e + RING < E:
                    gather(e + RING)
                add_rows(2 * e)
                add_rows(2 * e + 1)
            for k in range(2):
                pool.wait_ge(c_sc[k], 16 * CH * (E // 2))


def kernel(x, txt, L0_tok_W, L0_tok_b, L0_tok_cls_token, L0_tok_pos_emb, L0_attn_We1, L0_attn_be1,
           L0_attn_We2, L0_attn_be2, L0_attn_Wk1, L0_attn_bk1, L0_attn_Wk2, L0_attn_bk2, L0_ffn_Wr,
           L0_ffn_W1, L0_ffn_b1, L0_ffn_W2, L0_ffn_b2):
    import numpy as np
    import concourse.bacc as bacc
    from concourse.bass_utils import run_bass_kernel_spmd

    def a(v):
        return np.asarray(v)

    def tiles(v, n):
        return v.reshape((n, 128) + v.shape[1:]).swapaxes(0, 1)

    p = a(x).reshape(PAIRS, 2, 3, 11, 16, 13, 16).transpose(0, 4, 6, 2, 1, 3, 5)
    p = p.reshape(PAIRS, PK, 128, 2 * PATCHES).transpose(0, 2, 1, 3)
    pos = a(L0_tok_pos_emb).reshape(1 + PATCHES)
    pos2 = np.zeros((HALF, 2), pos.dtype)
    pos2[:, 0] = pos[:HALF]
    pos2[:IMG_ROWS1, 1] = pos[HALF:]
    w_up = np.concatenate([a(L0_attn_Wk1), a(L0_attn_We1)], 1).reshape(D, 4, 128)
    b_up = np.concatenate([a(L0_attn_bk1), a(L0_attn_be1)]).reshape(4, 128).T
    n = np.arange(128)
    ins = {
        "x": p,
        "txt": a(txt).reshape(PAIRS, 2, TXT, D).transpose(0, 2, 1, 3),
        "tok_w": tiles(a(L0_tok_W).T, PK),
        "tok_b": a(L0_tok_b).reshape(D, 1),
        "cls": a(L0_tok_cls_token).reshape(D, 1),
        "pos": pos2,
        "w_up": w_up,
        "b_up": b_up,
        "w_e2": tiles(a(L0_attn_We2), 2),
        "b_e2": np.broadcast_to(a(L0_attn_be2), (128, D)),
        "w_kq": tiles(a(L0_attn_Wk2), 2),
        "b_kq": a(L0_attn_bk2).reshape(128, 1),
        "wr": a(L0_ffn_Wr),
        "w1": a(L0_ffn_W1).transpose(1, 0, 2),
        "b1": a(L0_ffn_b1).reshape(E, FT, 128).transpose(2, 0, 1),
        "w2": a(L0_ffn_W2).reshape(E, FT, 128, D).transpose(2, 0, 1, 3),
        "b2": np.broadcast_to(a(L0_ffn_b2), (128, E, D)),
        "ident": np.eye(128, dtype=np.float32),
        "upto": (n[:HALF, None] <= n[None, :HALF]).astype(np.float32),
        "after": (n[:HALF, None] > n[None, :HALF]) + BIG * np.eye(HALF, dtype=np.float32),
        "before": (n[:, None] < n[None, :]).astype(np.float32),
        "group": (n[:, None] // GRP == n[None, :] // GRP).astype(np.float32),
        "rank": np.broadcast_to(np.arange(CAP, dtype=np.uint16), (128, CAP)),
        "number": np.concatenate([n[:, None] + 128 * np.arange(CH)[None, :],
                                  n[:, None] + 128 * np.arange(BLK)[None, :] > 0], 1).astype(np.float32),
    }
    ins = {"in_" + k: np.ascontiguousarray(v) for k, v in ins.items()}
    nc = bacc.Bacc("TRN2", target_bir_lowering=False, num_devices=1)
    args = [nc.dram_tensor(k, v.shape, mybir.dt.from_np(v.dtype), kind="ExternalInput").ap()
            for k, v in ins.items()]
    out = nc.dram_tensor("out", (IMGS, TOK, D), mybir.dt.float32, kind="ExternalOutput").ap()
    fusion_program(nc, *args, out)
    r = run_bass_kernel_spmd(nc, [ins], core_ids=[0])
    return r.results[0]["out"]
```
